# Optimizing a Trainium2 kernel written in Bass

```python
import numpy as np
import jax
import jax.numpy as jnp

def _softmax(x, axis=-1):
    return jax.nn.softmax(x, axis=axis)

def _gelu(x):
    return jax.nn.gelu(x, approximate=True)

def _silu(x):
    return jax.nn.silu(x)

def _sigmoid(x):
    return jax.nn.sigmoid(x)

def _layernorm(x, axis=-1, eps=1e-05):
    m = jnp.mean(x, axis=axis, keepdims=True)
    v = jnp.var(x, axis=axis, keepdims=True)
    return (x - m) / jnp.sqrt(v + eps)

def _scatter_add(tgt, idx, src, axis=0):
    return tgt.at[idx].add(src)

def _segment_sum(src, seg, n):
    return jax.ops.segment_sum(src, seg, n)
kernel_name = 'mk_sandwich_d1_jaxref_r4_fc5fcc'

def setup_inputs(seed: int=0):
    np.random.seed(seed)
    _w = jnp.asarray

    def _L0_attn_setup():
        import jax, jax.numpy as jnp
        import numpy as np
        N_HEAD = 16
        MA_K = 0.02
        LEAKY_SLOPE = 0.02
        NEG_INF = -1000000000.0

        def _heads(t, H):
            B, T, C = t.shape
            return t.reshape(B, T, H, C // H).transpose(0, 2, 1, 3)
        key = jax.random.key(seed)
        k1, k2, k3, k4 = jax.random.split(key, 4)
        B, T, C = (2, 512, 256)
        x = jax.random.normal(k1, (B, T, C), dtype=jnp.float32)
        s = 1.0 / np.sqrt(C)
        W_attn = jax.random.normal(k2, (C, 2 * C), dtype=jnp.float32) * s
        W_k2 = jax.random.normal(k3, (C, C), dtype=jnp.float32) * s
        W_proj = jax.random.normal(k4, (C, C), dtype=jnp.float32) * s
        return {'x': x, 'W_attn': W_attn, 'W_k2': W_k2, 'W_proj': W_proj}
    _L0_attn_in = _L0_attn_setup()

    def _L0_ffn_setup():
        import jax, jax.numpy as jnp
        import numpy as np
        DIM = 256
        HIDDEN = 768
        SCALE = 1.0 / 127.0

        def _dequant(w_int, dtype):
            return w_int.astype(dtype) * jnp.asarray(SCALE, dtype)
        key = jax.random.key(seed)
        k_x, k_g, k_u, k_d = jax.random.split(key, 4)
        x = jax.random.normal(k_x, (4, 512, DIM), dtype=jnp.float32)
        w_gate = jax.random.randint(k_g, (HIDDEN, DIM), -127, 128, dtype=jnp.int32)
        w_up = jax.random.randint(k_u, (HIDDEN, DIM), -127, 128, dtype=jnp.int32)
        w_down = jax.random.randint(k_d, (DIM, HIDDEN), -127, 128, dtype=jnp.int32)
        return {'x': x, 'w_gate': w_gate, 'w_up': w_up, 'w_down': w_down}
    _L0_ffn_in = _L0_ffn_setup()
    _d = {'L0_attn_x': _L0_attn_in['x'], 'L0_attn_W_attn': _L0_attn_in['W_attn'], 'L0_attn_W_k2': _L0_attn_in['W_k2'], 'L0_attn_W_proj': _L0_attn_in['W_proj'], 'L0_ffn_w_gate': _L0_ffn_in['w_gate'], 'L0_ffn_w_up': _L0_ffn_in['w_up'], 'L0_ffn_w_down': _L0_ffn_in['w_down']}
    _x0 = _d['L0_attn_x']
    _d['L0_attn_x'] = jax.random.normal(jax.random.fold_in(jax.random.key(seed), 1), (2, 2048, 256), dtype=_x0.dtype)
    del _x0
    return _d

def reference(L0_attn_x, L0_attn_W_attn, L0_attn_W_k2, L0_attn_W_proj, L0_ffn_w_gate, L0_ffn_w_up, L0_ffn_w_down):

    def _L0_attn_ref(x, W_attn, W_k2, W_proj):
        import jax, jax.numpy as jnp
        import numpy as np
        N_HEAD = 16
        MA_K = 0.02
        LEAKY_SLOPE = 0.02
        NEG_INF = -1000000000.0

        def _heads(t, H):
            B, T, C = t.shape
            return t.reshape(B, T, H, C // H).transpose(0, 2, 1, 3)
        B, T, C = x.shape
        H = N_HEAD
        d = C // H
        scale = 1.0 / jnp.sqrt(jnp.asarray(d, x.dtype))
        qk = x @ W_attn
        q, k = jnp.split(qk, 2, axis=-1)
        q = _heads(q, H)
        k = _heads(k, H)
        v = _heads(x, H)
        scores = jnp.einsum('bhtd,bhsd->bhts', q, k) * scale
        causal = jnp.tril(jnp.ones((T, T), dtype=bool))
        scores = jnp.where(causal, scores, NEG_INF)
        attn = jax.nn.softmax(scores, axis=-1)
        y = jnp.einsum('bhts,bhsd->bhtd', attn, v)
        e = v[:, :, 1:, :] - y[:, :, :-1, :]
        k2 = _heads(x[:, :-1, :] @ W_k2, H)
        q2 = q[:, :, 1:, :]
        qa = -jax.nn.leaky_relu(-q2 * scale, negative_slope=LEAKY_SLOPE)
        ka = jax.nn.sigmoid(MA_K * (k2 * scale))
        w = jnp.einsum('bhtd,bhsd->bhts', qa, ka)
        w = jnp.tril(w)
        y2 = jnp.einsum('bhts,bhsd->bhtd', w, e)
        y2 = jnp.concatenate([jnp.zeros_like(y2[:, :, :1, :]), y2], axis=2)

        def merge(t):
            return t.transpose(0, 2, 1, 3).reshape(B, T, C)
        return merge(y) @ W_proj + merge(y2) @ W_proj

    def _L0_ffn_ref(x, w_gate, w_up, w_down):
        import jax, jax.numpy as jnp
        import numpy as np
        DIM = 256
        HIDDEN = 768
        SCALE = 1.0 / 127.0

        def _dequant(w_int, dtype):
            return w_int.astype(dtype) * jnp.asarray(SCALE, dtype)
        wg = _dequant(w_gate, x.dtype)
        wu = _dequant(w_up, x.dtype)
        wd = _dequant(w_down, x.dtype)
        gate = jnp.einsum('bsd,hd->bsh', x, wg)
        up = jnp.einsum('bsd,hd->bsh', x, wu)
        h = jax.nn.silu(gate) * up
        return jnp.einsum('bsh,dh->bsd', h, wd)
    x = L0_attn_x
    x = x + _layernorm(_L0_attn_ref(_layernorm(x, axis=-1), L0_attn_W_attn, L0_attn_W_k2, L0_attn_W_proj), axis=-1)
    x = x + _layernorm(_L0_ffn_ref(_layernorm(x, axis=-1), L0_ffn_w_gate, L0_ffn_w_up, L0_ffn_w_down), axis=-1)
    return x

_drawn_inputs = setup_inputs


def setup_inputs(seed=0):
    import zlib

    import numpy as np

    out = dict(_drawn_inputs(seed))
    spreads = {}
    factors = {'L0_attn_W_k2': 64.0}
    for name, (base, spread) in spreads.items():
        noise = np.random.default_rng([zlib.crc32(name.encode()), seed]).standard_normal(out[name].shape)
        drawn = base * np.exp(spread * noise) if base else spread * noise
        out[name] = jnp.asarray(drawn.astype(out[name].dtype))
    for name, factor in factors.items():
        out[name] = (out[name] * factor).astype(out[name].dtype)
    return out
```

```python
from contextlib import ExitStack

import concourse.bass as bass
from concourse import mybir

P = 128
BLK = 512
TPB = BLK // P
B, T, C = 2, 2048, 256
NTOK = B * T
NBLK = NTOK // BLK
NQ = T // BLK
H, D = 16, 16
HG = 4
CG = HG * D
HID = 768
NH = HID // P
KT = C // P
PAD = 32
TERMS = ((0, 0), (0, 1), (1, 0), (0, 2), (2, 0), (1, 1))
ROWS = D * len(TERMS)
NM = 3
SCALE = 1.0 / D ** 0.5
MA_SCALE = 0.02 * SCALE
LEAK = 0.02 * SCALE
WSCALE = 1.0 / 127.0
EPS = 1e-5
SAFE = 75.0
NEG = -1e30

ALU = mybir.AluOpType
ACT = mybir.ActivationFunctionType
F32, BF16, F16, I32 = mybir.dt.float32, mybir.dt.bfloat16, mybir.dt.float16, mybir.dt.int32
AX = mybir.AxisListType
ds = bass.ds


def hold(engine, sem, value, idle):
    if not isinstance(value, int) or value > 0:
        engine.wait_ge(sem, value)
        engine.sem_inc(idle, 1)


class Steps:

    def __init__(self, engine, sem, base=0):
        self.engine, self.sem, self.base, self.n = engine, sem, base, 0

    def link(self, ins, idle=None):
        self.n += 1
        ins.then_inc(self.sem, 1)
        if idle is None:
            self.engine.wait_ge(self.sem, self.base + self.n)
        else:
            hold(self.engine, self.sem, self.base + self.n, idle)


LN_STEPS = 14


def ln_moments(nc, chain, rows, st, mv, idle):
    for i, row in enumerate(rows):
        ins = nc.vector.bn_stats(st[:, i, :], row)
    chain.link(ins, idle)
    for i in range(len(rows)):
        ins = nc.vector.bn_aggr(mv[:, i, :], st[:, i, :])
    chain.link(ins)


def ln_rsqrt(nc, chain, mv, nt):
    v, y, t = nt
    chain.link(nc.vector.tensor_scalar(v[:], mv[:, :, 1], EPS, None, ALU.add))
    chain.link(nc.vector.tensor_scalar(t[:].bitcast(I32), v[:].bitcast(I32), 1, None, ALU.logical_shift_right))
    chain.link(nc.vector.tensor_scalar(y[:].bitcast(I32), t[:].bitcast(I32), -1.0, float(0x5F3759DF), ALU.mult, ALU.add))
    for k in range(3):
        chain.link(nc.vector.tensor_tensor(t[:], y[:], y[:], ALU.mult))
        chain.link(nc.vector.scalar_tensor_tensor(t[:], t[:], -0.5, v[:], ALU.mult, ALU.mult))
        out = y[:] if k < 2 else mv[:, :, 1]
        chain.link(nc.vector.scalar_tensor_tensor(out, t[:], 1.5, y[:], ALU.add, ALU.mult))


def project(nc, x, w_qk, w_k2, ident, heads, flag, parts, qa32, ka_nat, xn_dram):
    Q, K, KA, QA = 0, 2, 4, 6
    with ExitStack() as ctx:
        sb = lambda name, shape, dt: ctx.enter_context(nc.sbuf_tensor(name, shape, dt))
        ps = lambda name, shape: ctx.enter_context(nc.psum_tensor(name, shape, F32))
        sem = lambda name: ctx.enter_context(nc.semaphore(name))
        w = sb("w_all", [P, KT, 3 * C], F32)
        idf = sb("ident_a", [P, P], F32)
        ind = sb("head_of_channel", [P, P // D], F32)
        x4 = sb("x_block", [P, TPB, C], F32)
        xs = sb("xn_block", [P, TPB, C], F32)
        xt = sb("xn_t", [P, KT, BLK], F32)
        hi_lo = sb("parts_sb", [P, 8, 3, BLK], BF16)
        rest = sb("rest", [P, 8, BLK], F32)
        small = sb("q_leak", [P, 2, BLK], F32)
        qaf = sb("qa_f32", [P, 2, BLK], F32)
        kaf = sb("ka_f32", [P, 2, BLK], F32)
        kn = sb("ka_nat_sb", [P, TPB, C], F32)
        zrow = sb("zero_row", [1, CG], F32)
        st = sb("st_a", [P, TPB, 6], F32)
        mv = sb("mv_a", [P, TPB, 2], F32)
        nt = [sb(f"nt_a{i}", [P, TPB], F32) for i in range(3)]
        peak = sb("peak", [P, 8, BLK], BF16)
        top = sb("peak_top", [P, 8], F32)
        prod = sb("peak_prod", [P, 2], F32)
        bound = sb("bound", [1, 1], F32)
        xt_ps = ps("xt_ps", [P, KT, BLK])
        u = ps("u_ps", [P, 4, BLK])
        kn_ps = ps("kn_ps", [P, TPB, C])

        idle = sem("idle_a")
        w_in, x_in, xn_done, xt_up, xt_down = sem("w_in"), sem("x_in"), sem("xn_done"), sem("xt_up"), sem("xt_down")
        u_ready, u_read = sem("u_ready"), sem("u_read")
        hi_ready, leak_ready, kaf_ready, qaf_ready = sem("hi_ready"), sem("leak_ready"), sem("kaf_ready"), sem("qaf_ready")
        rest_ready, mid_ready, lo_dve, lo_pool = sem("rest_ready"), sem("mid_ready"), sem("lo_dve"), sem("lo_pool")
        kn_up, kn_down = sem("kn_up"), sem("kn_down")
        stored = [sem(f"stored{s}") for s in range(8)]
        qa_stored, kn_stored, xn_stored, z_stored = [sem("qa_stored0"), sem("qa_stored1")], sem("kn_stored"), sem("xn_stored"), sem("z_stored")
        chain_s, peak_done, prod_ready, sum_ready, z_ready, bound_ready = sem("chain_a"), sem("peak_done"), sem("prod_ready"), sem("sum_ready"), sem("z_ready"), sem("bound_ready")

        def tokens(dram, n, g):
            return dram[ds((n // NQ * (C // CG) + g) * T + n % NQ * BLK, BLK), :].rearrange("(i p) c -> p i c", p=P)

        def load_x(sp, n):
            sp.dma_start(x4[:], x[ds(n * BLK, BLK), :].rearrange("(i p) c -> p i c", p=P)).then_inc(x_in, 16)

        with nc.Block() as block:

            @block.sync
            def _(sp):
                load_x(sp, 0)
                sp.dma_start(idf[:], ident).then_inc(w_in, 16)
                sp.dma_start(w[:, :, 0:2 * C], w_qk.rearrange("(k p) m -> p k m", p=P)).then_inc(w_in, 16)
                sp.dma_start(w[:, :, 2 * C:], w_k2.rearrange("(k p) m -> p k m", p=P)).then_inc(w_in, 16)
                sp.dma_start(ind[:], heads).then_inc(w_in, 16)
                sp.wait_ge(z_ready, 1)
                sp.dma_start(xn_dram[NTOK * C // CG:, :], zrow[:]).then_inc(z_stored, 16)
                for s in stored + qa_stored:
                    sp.sem_inc(s, 16)
                sp.sem_inc(kn_stored, 64)

                def body(n, more):
                    if more:
                        hold(sp, xn_done, 4 * n + 4, idle)
                        load_x(sp, n + 1)
                    hold(sp, xn_done, 4 * n + 4, idle)
                    for g in range(C // CG):
                        sp.dma_start(tokens(xn_dram, n, g), xs[:, :, g * CG:(g + 1) * CG]).then_inc(xn_stored, 16)
                    for s in range(8):
                        if s < 4:
                            hold(sp, lo_dve, 4 * n + s + 1, idle)
                        else:
                            hold(sp, lo_pool, 4 * n + s - 3, idle)
                        sp.dma_start(parts[s // 2, :, ds(n // NQ * C + s % 2 * P, P), ds(n % NQ * BLK, BLK)].rearrange("a p t -> p a t"),
                                     hi_lo[:, s]).then_inc(stored[s], 16)
                        if s == 1:
                            for c in range(2):
                                hold(sp, qaf_ready, 2 * n + c + 1, idle)
                                sp.dma_start(qa32[ds(n // NQ * C + c * P, P), ds(n % NQ * BLK, BLK)], qaf[:, c]).then_inc(qa_stored[c], 16)
                    hold(sp, kn_down, n + 2, idle)
                    for g in range(C // CG):
                        sp.dma_start(tokens(ka_nat, n, g), kn[:, :, g * CG:(g + 1) * CG]).then_inc(kn_stored, 16)

                with sp.Fori(0, NBLK - 1) as n:
                    body(n, True)
                body(NBLK - 1, False)
                for s in stored + qa_stored:
                    sp.wait_ge(s, 16 * NBLK + 16)
                sp.wait_ge(kn_stored, 64 * NBLK + 64)
                sp.wait_ge(xn_stored, 64 * NBLK)
                sp.wait_ge(z_stored, 16)

            @block.vector
            def _(dve):
                nc.vector.memset(zrow[:], 0.0).then_inc(z_ready, 1)
                nc.vector.memset(peak[:], 0.0).then_inc(peak_done, 1)
                dve.sem_inc(u_read, 4)
                dve.sem_inc(rest_ready, 8)

                def norm(n):
                    dve.wait_ge(x_in, 16 * n + 16)
                    chain = Steps(dve, chain_s, n * LN_STEPS)
                    ln_moments(nc, chain, [x4[:, i, :] for i in range(TPB)], st, mv, idle)
                    ln_rsqrt(nc, chain, mv, nt)
                    assert chain.n == LN_STEPS
                    if not (isinstance(n, int) and n == 0):
                        dve.wait_ge(xt_up, n)
                        dve.wait_ge(xn_stored, 64 * n)
                    for i in range(TPB):
                        nc.vector.tensor_scalar(xs[:, i, :], x4[:, i, :],
                                                mv[:, i, 0:1], mv[:, i, 1:2], ALU.subtract, ALU.mult).then_inc(xn_done, 1)

                def lo(n, s):
                    dve.wait_ge(mid_ready, 8 * n + s + 1)
                    nc.vector.tensor_tensor(hi_lo[:, s, 2], rest[:, s], hi_lo[:, s, 1], ALU.subtract).then_inc(lo_dve, 1)

                def body(n, more):
                    for s in range(4):
                        dve.wait_ge(hi_ready, 8 * n + s + 1)
                        if s < 2:
                            dve.wait_ge(leak_ready, 2 * n + s + 1)
                        nc.vector.tensor_tensor(rest[:, s], u[:, s], hi_lo[:, s, 0], ALU.subtract).then_inc(rest_ready, 1)
                        if s < 2:
                            dve.wait_ge(qa_stored[s], 16 * n + 16)
                            dve.wait_ge(rest_ready, 8 * n + 7 + s)
                            nc.vector.scalar_tensor_tensor(qaf[:, s], u[:, s], SCALE, small[:, s], ALU.mult, ALU.min).then_inc(qaf_ready, 1)
                        dve.wait_ge(peak_done, 4 * n + s + 1)
                        nc.vector.tensor_tensor(peak[:, s], hi_lo[:, s, 0], peak[:, s], ALU.max)
                        nc.vector.tensor_tensor(peak[:, 4 + s], hi_lo[:, s, 0], peak[:, 4 + s], ALU.min).then_inc(peak_done, 1)
                        if s >= 2:
                            lo(n, s - 2)
                    if more:
                        norm(n + 1)
                    for s in range(4, 8):
                        dve.wait_ge(hi_ready, 8 * n + s + 1)
                        f = kaf[:, s - 4] if s < 6 else qaf[:, s - 6]
                        nc.vector.tensor_tensor(rest[:, s], f, hi_lo[:, s, 0], ALU.subtract).then_inc(rest_ready, 1)
                        if s < 6:
                            lo(n, s - 2)

                norm(0)
                with dve.Fori(0, NBLK - 1) as n:
                    body(n, True)
                body(NBLK - 1, False)
                dve.wait_ge(peak_done, 4 * NBLK + 1)
                nc.vector.tensor_reduce(top[:, 0:4], peak[:, 0:4], AX.X, ALU.max)
                nc.vector.tensor_reduce(top[:, 4:8], peak[:, 4:8], AX.X, ALU.min).then_inc(peak_done, 1)
                dve.wait_ge(peak_done, 4 * NBLK + 2)
                nc.vector.scalar_tensor_tensor(top[:, 0:4], top[:, 4:8], -1.0, top[:, 0:4], ALU.mult, ALU.max).then_inc(prod_ready, 1)
                dve.wait_ge(prod_ready, 1)
                nc.vector.tensor_tensor(prod[:], top[:, 0:2], top[:, 2:4], ALU.mult).then_inc(prod_ready, 1)
                dve.wait_ge(sum_ready, 1)
                nc.vector.tensor_reduce(bound[:], kn_ps[0:1, 0, 0:KT * P // D], AX.X, ALU.max).then_inc(bound_ready, 1)
                dve.wait_ge(bound_ready, 1)
                nc.vector.tensor_scalar(flag[:], bound[:], SCALE * 1.01, SAFE, ALU.mult, ALU.is_gt).then_inc(bound_ready, 1)

            @block.scalar
            def _(act):
                act.sem_inc(kaf_ready, 2)
                act.sem_inc(kn_down, 1)

                def xt_evac(n):
                    act.wait_ge(xt_up, n + 1)
                    act.wait_ge(u_ready, 6 * n + 1)
                    nc.scalar.copy(xt[:], xt_ps[:]).then_inc(xt_down, 1)

                def hi(n, s, src):
                    act.wait_ge(stored[s], 16 * n + 16)
                    nc.scalar.copy(hi_lo[:, s, 0], src).then_inc(hi_ready, 1)

                def body(n, more):
                    for s in range(4):
                        act.wait_ge(u_ready, 6 * n + s + 2)
                        hi(n, s, u[:, s])
                        if s < 2:
                            nc.scalar.mul(small[:, s], u[:, s], LEAK).then_inc(leak_ready, 1)
                    for s in range(2):
                        act.wait_ge(u_ready, 6 * n + s + 6)
                        act.wait_ge(rest_ready, 8 * n + s + 5)
                        nc.scalar.activation(kaf[:, s], u[:, s], ACT.Sigmoid, scale=MA_SCALE).then_inc(kaf_ready, 1)
                    if more:
                        xt_evac(n + 1)
                    act.wait_ge(kaf_ready, 2 * n + 4)
                    for s in range(4, 6):
                        hi(n, s, kaf[:, s - 4])
                    for s in range(6, 8):
                        act.wait_ge(qaf_ready, 2 * n + s - 5)
                        hi(n, s, qaf[:, s - 6])
                    act.wait_ge(kn_up, n + 1)
                    act.wait_ge(kn_stored, 64 * n + 64)
                    nc.scalar.copy(kn[:], kn_ps[:]).then_inc(kn_down, 1)

                xt_evac(0)
                with act.Fori(0, NBLK - 1) as n:
                    body(n, True)
                body(NBLK - 1, False)

            @block.gpsimd
            def _(pool):
                def body(n):
                    for s in range(8):
                        hold(pool, rest_ready, 8 * n + 8 + s + 1, idle)
                        nc.gpsimd.tensor_copy(hi_lo[:, s, 1], rest[:, s]).then_inc(mid_ready, 1)
                        if s >= 4:
                            pool.wait_ge(mid_ready, 8 * n + s + 1)
                            nc.gpsimd.tensor_tensor(hi_lo[:, s, 2], rest[:, s], hi_lo[:, s, 1], ALU.subtract).then_inc(lo_pool, 1)

                with pool.Fori(0, NBLK) as n:
                    body(n)

            @block.tensor
            def _(pe):
                pe.sem_inc(u_ready, 1)

                def turn_x(n):
                    pe.wait_ge(xn_done, 4 * n + 4)
                    if not (isinstance(n, int) and n == 0):
                        pe.wait_ge(xt_down, n)
                    for i in range(TPB):
                        for k in range(KT):
                            last = nc.tensor.transpose(xt_ps[:, k, i * P:i * P + P], xs[:, i, k * P:k * P + P], idf[:])
                    last.then_inc(xt_up, 1)

                def tile(n, m):
                    if m == 0:
                        pe.wait_ge(kaf_ready, 2 * n + 1)
                    elif m == 1:
                        pe.wait_ge(kaf_ready, 2 * n + 2)
                    elif m < 4:
                        pe.wait_ge(rest_ready, 8 * n + m + 1)
                    else:
                        pe.wait_ge(qaf_ready, 2 * n + m - 3)
                    for k in range(KT):
                        ins = nc.tensor.matmul(u[:, m % 4], w[:, k, m * P:m * P + P], xt[:, k], start=(k == 0), stop=(k == KT - 1))
                    ins.then_inc(u_ready, 1)

                def body(n, more):
                    pe.wait_ge(xt_down, n + 1)
                    for m in range(6):
                        tile(n, m)
                    if more:
                        turn_x(n + 1)
                    pe.wait_ge(kaf_ready, 2 * n + 4)
                    pe.wait_ge(kn_down, n + 1)
                    for i in range(TPB):
                        for k in range(KT):
                            last = nc.tensor.transpose(kn_ps[:, i, k * P:k * P + P], kaf[:, k, i * P:i * P + P], idf[:])
                    last.then_inc(kn_up, 1)

                pe.wait_ge(w_in, 64)
                turn_x(0)
                with pe.Fori(0, NBLK - 1) as n:
                    body(n, True)
                body(NBLK - 1, False)
                pe.wait_ge(prod_ready, 2)
                pe.wait_ge(kn_down, NBLK + 1)
                for k in range(KT):
                    last = nc.tensor.matmul(kn_ps[0:1, 0, k * (P // D):(k + 1) * (P // D)], prod[:, k:k + 1], ind[:], start=True, stop=True)
                last.then_inc(sum_ready, 1)


NG = B * C // CG
UB = [4 * n * (n + 1) // 2 for n in range(NQ + 1)]
UNITS = UB[NQ]
SHORT = {0: ["A0"], 1: ["T"], 2: ["A1", "G"], 3: ["A2", "Y", "A3", "Z"]}
LONG = {0: ["A0"], 1: ["T"], 2: ["A1"], 3: ["G", "A2"], 4: ["A3"], 5: ["Y"], 7: ["Z"]}
W_USES = 6
LAST = "TGYZ"


def attend(nc, cst, flag, z, parts, qa32, ka_nat, xn_dram, rows_dram):
    with ExitStack() as ctx:
        sb = lambda name, shape, dt: ctx.enter_context(nc.sbuf_tensor(name, shape, dt))
        ps = lambda name, shape: ctx.enter_context(nc.psum_tensor(name, shape, F32))
        sem = lambda name: ctx.enter_context(nc.semaphore(name))
        idf = sb("ident_f", [P, P], F32)
        idb = sb("ident_b", [P, P], BF16)
        later = sb("later_keys", [P, P], BF16)
        later_t = sb("later_keys_t", [P, P], BF16)
        before = sb("before", [P, P], F32)
        own = sb("own_head", [CG, P], F32)
        ks = sb("k_stack", [ROWS + NM, 2, HG, T], BF16)
        qs = sb("q_stack", [ROWS + NM, NQ, HG, BLK], BF16)
        kas = sb("ka_stack", [ROWS, 2, HG, BLK], BF16)
        qas = sb("qa_stack", [ROWS, 2, HG, BLK], BF16)
        qap = sb("qa_plain", [CG, 2, BLK], F32)
        kan = sb("ka_tokens", [P, 2, TPB, CG], F32)
        vnext = sb("v_next", [P, 2, TPB, CG], F32)
        vraw = sb("v_raw", [P, T // P, CG], F32)
        va = sb("v_and_one", [P, 2, T // P, HG, PAD], F32)
        pr = sb("probs", [P, 4, 2, BLK], F32)
        am = sb("local_products", [P, 2, TPB, HG, P], F32)
        e = sb("e_padded", [P, TPB, HG, PAD], F32)
        ot = sb("y_t", [P, BLK], F32)
        y2t = sb("y2_t", [P, BLK], F32)
        inv = sb("inv_sum", [P, TPB, HG], F32)
        y = sb("y_tokens", [P, TPB, HG, D], F32)
        run = sb("running", [CG, TPB + 1, P], F32)
        gm = sb("ka_e", [CG, TPB, P], F32)
        nmax = sb("minus_max", [P, HG * TPB], F32)
        nsplit = sb("minus_max_rest", [HG * TPB, P], F32)
        nrow = sb("minus_max_parts", [HG * TPB, NM, P], BF16)
        s_ps = ps("s_ps", [P, 4, BLK])
        o_ps = [ps(f"o_ps{i}", [P, BLK]) for i in range(2)]
        w_ps = ps("w_ps", [P, BLK])
        x_ps = ps("x_ps", [P, BLK])

        idle = sem("idle_b")
        consts_in, pads_ready, stacks_ready = sem("consts_in"), sem("pads_ready"), sem("stacks_ready")
        ks_in = [sem(f"ks_in{i}") for i in range(2)]
        qs_in = [sem(f"qs_in{i}") for i in range(NQ)]
        as_in = [sem(f"as_in{i}") for i in range(2)]
        lin_in = [sem(f"lin_in{i}") for i in range(2)]
        v_in, va_ready = sem("v_in"), sem("va_ready")
        scores_up, probs_ready, pv_done, o_read = sem("scores_up"), sem("probs_ready"), sem("pv_done"), sem("o_read")
        w_up, w_read, x_up, x_read = sem("w_up"), sem("w_read"), sem("x_up"), sem("x_read")
        e_ready, run_ready, chain_s = sem("e_ready"), sem("run_ready"), sem("chain_b")
        m_up, m_read, mt_up, mt_parts, m_out, m_rows, m_chain = sem("m_up"), sem("m_read"), sem("mt_up"), sem("mt_parts"), sem("m_out"), sem("m_rows"), sem("m_chain")

        def at_least(engine, s, value):
            if not isinstance(value, int) or value > 0:
                engine.wait_ge(s, value)

        def groups(engine, group):
            group(0, 0, 0)
            with engine.Fori(0, (NG - 2) // 2) as i:
                group(2 * i + 1, 1, i)
                group(2 * i + 2, 0, i + 1)
            group(NG - 1, 1, (NG - 1) // 2)

        def tasks(it, n, u):
            very_first = isinstance(it, int) and it == 0 and n == 0
            wn = 0 if very_first else W_USES * (4 * it + n) - 2
            xn_ = 0 if very_first else 2 * (4 * it + n) - 2
            out = []
            for uu, names in sorted((SHORT if n == 0 else LONG).items()):
                for name in names:
                    if very_first and name in LAST:
                        continue
                    if uu == u:
                        out.append((name, wn, xn_))
                    if name in "GY":
                        xn_ += 1
                    else:
                        wn += 1
            return out

        W_END, X_END = W_USES * 4 * NG - 2, 2 * 4 * NG - 2

        with nc.Block() as block:

            @block.sync
            def _(sp):
                for dst, name in ((idf, "ident"), (idb, "ident_bf"), (later, "later"), (later_t, "later_t"), (before, "before"), (own, "own")):
                    sp.dma_start(dst[:], cst[name]).then_inc(consts_in, 16)

                def stack(dst, kind, side, it, cols, s):
                    for r, term in enumerate(TERMS):
                        sp.dma_start(dst[r * D:(r + 1) * D],
                                     parts[kind, term[side], ds(it * CG, CG), cols].rearrange("(j d) t -> d j t", d=D)).then_inc(s, 16)

                def group(it, slot, rnd):
                    hold(sp, pv_done, UNITS * it - UNITS + 1, idle)
                    stack(ks[:, slot], 1, 0, it, slice(0, T), ks_in[slot])
                    hold(sp, va_ready, it, idle)
                    sp.dma_start(vraw[:], xn_dram[ds(it * T, T), :].rearrange("(i p) c -> p i c", p=P)).then_inc(v_in, 16)
                    for n in range(NQ):
                        bx = 4 * it + n
                        cols = slice(n * BLK, n * BLK + BLK)
                        hold(sp, pv_done, UNITS * it - UNITS + UB[n + 1], idle)
                        stack(qs[:, n], 0, 1, it, cols, qs_in[n])
                        hold(sp, w_read, W_USES * bx - W_USES - 2 if not (isinstance(it, int) and bx < 2) else 0, idle)
                        stack(kas[:, n % 2], 2, 0, it, cols, as_in[n % 2])
                        stack(qas[:, n % 2], 3, 1, it, cols, as_in[n % 2])
                        hold(sp, x_read, 2 * bx - 2, idle)
                        sp.dma_start(qap[:, n % 2], qa32[ds(it * CG, CG), cols]).then_inc(lin_in[n % 2], 16)
                        sp.dma_start(kan[:, n % 2], ka_nat[ds(it * T + n * BLK, BLK), :].rearrange("(i p) c -> p i c", p=P)).then_inc(lin_in[n % 2], 16)
                        sp.dma_start(vnext[:, n % 2], xn_dram[ds(it * T + n * BLK + 1, BLK), :].rearrange("(i p) c -> p i c", p=P)).then_inc(lin_in[n % 2], 16)

                groups(sp, group)

            @block.gpsimd
            def _(pool):
                nc.gpsimd.memset(va[:], 0.0).then_inc(pads_ready, 1)
                nc.gpsimd.memset(e[:], 0.0).then_inc(pads_ready, 1)
                pool.wait_ge(pads_ready, 1)
                for slot in range(2):
                    nc.gpsimd.memset(va[:, slot, :, :, D:D + 1], 1.0).then_inc(pads_ready, 1)

                def values(it, slot):
                    pool.wait_ge(v_in, 16 * it + 16)
                    hold(pool, pv_done, UNITS * it - UNITS, idle)
                    nc.gpsimd.tensor_copy(va[:, slot, :, :, 0:D], vraw[:].rearrange("p i (j d) -> p i j d", d=D)).then_inc(va_ready, 1)

                def next_minus_y(bx, n, w_use):
                    pool.wait_ge(w_read, w_use + 1)
                    pool.wait_ge(lin_in[n % 2], 24 * bx - 24 * (n % 2) + 48)
                    nc.gpsimd.tensor_tensor(e[:, :, :, 0:D], vnext[:, n % 2].rearrange("p i (j d) -> p i j d", d=D), y[:], ALU.subtract).then_inc(e_ready, 1)

                def group(it, slot, rnd):
                    for n in range(NQ):
                        for u in range(4 * n + 4):
                            for name, wn, xn_ in tasks(it, n, u):
                                if name == "T":
                                    next_minus_y(4 * it + n - 1, (n - 1) % NQ, wn)
                        if n == NQ - 1 and not (isinstance(it, int) and it == NG - 1):
                            values(it + 1, 1 - slot)

                values(0, 0)
                groups(pool, group)
                next_minus_y(4 * NG - 1, NQ - 1, W_END)

            @block.scalar
            def _(act):
                slow = act.value_load(flag[0:1, 0:1], min_val=0, max_val=1)

                def group(it, slot, rnd):
                    for n in range(NQ):
                        with act.If(slow > 0):
                            act.wait_ge(mt_parts, 12 * it + 3 * n + 3)
                            act.dma_start(rows_dram.rearrange("k (r t) -> r k t", t=P), nrow[:]).then_inc(m_out, 16)
                            act.wait_ge(m_out, 64 * it + 16 * n + 16)
                            act.dma_start(qs[ROWS:ROWS + NM, n], rows_dram.rearrange("k (j t) -> k j t", j=HG)).then_inc(m_rows, 16)
                        for u in range(4 * n + 4):
                            unit = UNITS * it + UB[n] + u
                            t0 = max(0, (u - 4 * n) * P)
                            for h in range(2):
                                act.wait_ge(scores_up, 2 * unit + h + 1)
                                at_least(act, pv_done, unit - 1)
                                nc.scalar.activation(pr[:, 2 * (u % 2) + h, :, t0:], s_ps[:, 2 * h:2 * h + 2, t0:], ACT.Exp, scale=SCALE).then_inc(probs_ready, 1)

                groups(act, group)

            @block.vector
            def _(dve):
                slow = dve.value_load(flag[0:1, 0:1], min_val=0, max_val=1)
                nc.vector.memset(qs[ROWS:ROWS + NM], 0.0).then_inc(stacks_ready, 1)
                nc.vector.memset(ks[ROWS:ROWS + NM], 1.0).then_inc(stacks_ready, 1)
                dve.wait_ge(consts_in, 96)

                def maxima(it, n, slot):
                    bx = 4 * it + n
                    for i in range(TPB):
                        for j in range(HG):
                            dve.wait_ge(m_up, 16 * bx + 4 * i + j + 1)
                            width = (4 * n + i + 1) * P
                            ins = nc.vector.tensor_reduce(nmax[:, j * TPB + i:j * TPB + i + 1],
                                                          s_ps[:].rearrange("p a t -> p (a t)")[:, 0:width], AX.X, ALU.max, negate=True)
                            ins.then_inc(m_read, 1)
                    dve.wait_ge(mt_up, bx + 1)
                    at_least(dve, m_rows, 16 * bx)
                    turned = w_ps[0:HG * TPB, 0:P]
                    nc.vector.tensor_copy(nrow[:, 0], turned).then_inc(mt_parts, 1)
                    dve.wait_ge(mt_parts, 3 * bx + 1)
                    nc.vector.tensor_tensor(nsplit[:], turned, nrow[:, 0], ALU.subtract).then_inc(m_chain, 1)
                    dve.wait_ge(m_chain, bx + 1)
                    nc.vector.tensor_copy(nrow[:, 1], nsplit[:]).then_inc(mt_parts, 1)
                    dve.wait_ge(mt_parts, 3 * bx + 2)
                    nc.vector.tensor_tensor(nrow[:, 2], nsplit[:], nrow[:, 1], ALU.subtract).then_inc(mt_parts, 1)

                def o_evac(bx, par, unit_end):
                    dve.wait_ge(pv_done, unit_end)
                    nc.vector.tensor_copy(ot[:], o_ps[par][:]).then_inc(o_read, 1)

                def task(name, bx, n, wn, xn_):
                    if name[0] == "A":
                        c = int(name[1])
                        dve.wait_ge(w_up, wn + 1)
                        nc.vector.tensor_tensor(am[:, n % 2, c], w_ps[:].rearrange("p (j t) -> p j t", j=HG),
                                                before[:].unsqueeze(1).to_broadcast([P, HG, P]), ALU.mult).then_inc(w_read, 1)
                    elif name == "T":
                        dve.wait_ge(w_up, wn + 1)
                        o4 = w_ps[:].rearrange("p (i j c) -> p i j c", i=TPB, j=HG)
                        at_least(dve, w_read, wn)
                        nc.vector.reciprocal(inv[:], o4[:, :, :, D]).then_inc(chain_s, 1)
                        dve.wait_ge(chain_s, 2 * bx + 1)
                        nc.vector.tensor_tensor(y[:], o4[:, :, :, 0:D], inv[:].unsqueeze(3).to_broadcast([P, TPB, HG, D]), ALU.mult).then_inc(w_read, 1)
                    elif name == "G":
                        dve.wait_ge(x_up, xn_ + 1)
                        at_least(dve, run_ready, 4 * bx)
                        nc.vector.tensor_tensor(gm[:], x_ps[0:CG].rearrange("p (i c) -> p i c", i=TPB),
                                                own[:].unsqueeze(1).to_broadcast([CG, TPB, P]), ALU.mult).then_inc(x_read, 1)
                        if n == 0:
                            nc.vector.memset(run[:, 0], 0.0).then_inc(chain_s, 1)
                        else:
                            nc.vector.tensor_copy(run[:, 0], run[:, TPB]).then_inc(chain_s, 1)
                        dve.wait_ge(x_read, xn_ + 1)
                        dve.wait_ge(chain_s, 2 * bx + 2)
                        for c in range(TPB):
                            if c:
                                dve.wait_ge(run_ready, 4 * bx + c)
                            nc.vector.tensor_tensor(run[:, c + 1], run[:, c], gm[:, c], ALU.add).then_inc(run_ready, 1)
                    elif name == "Y":
                        dve.wait_ge(x_up, xn_ + 1)
                        nc.vector.tensor_copy(y2t[:], x_ps[:]).then_inc(x_read, 1)
                    else:
                        dve.wait_ge(w_up, wn + 1)
                        grp = bx // 4
                        o4 = w_ps[:].rearrange("p (i j c) -> p i j c", i=TPB, j=HG)
                        out = z[:, ds(grp * (T // P) + 4 * n, TPB), :].rearrange("p i (j d) -> p i j d", d=D)
                        nc.vector.tensor_tensor(out, o4[:, :, :, 0:D], y[:], ALU.add).then_inc(w_read, 1)

                def group(it, slot, rnd):
                    for n in range(NQ):
                        bx = 4 * it + n
                        with dve.If(slow > 0):
                            maxima(it, n, slot)
                        for u in range(4 * n + 4):
                            if u == 0 and not (isinstance(bx, int) and bx == 0):
                                o_evac(bx - 1, (n - 1) % 2, UNITS * it + UB[n])
                            for name, wn, xn_ in tasks(it, n, u):
                                if name[0] == "A":
                                    task(name, bx, n, wn, xn_)
                                else:
                                    task(name, bx - 1, (n - 1) % NQ, wn, xn_)

                groups(dve, group)
                o_evac(4 * NG - 1, 1, UNITS * NG)
                wn, xn_ = W_END, X_END
                for name in LAST:
                    task(name, 4 * NG - 1, NQ - 1, wn, xn_)
                    wn, xn_ = wn + (name in "TZ"), xn_ + (name in "GY")

            @block.tensor
            def _(pe):
                slow = pe.value_load(flag[0:1, 0:1], min_val=0, max_val=1)
                pe.wait_ge(consts_in, 96)
                pe.wait_ge(pads_ready, 4)

                def maxima(it, n, slot):
                    bx = 4 * it + n
                    at_least(pe, probs_ready, 2 * (UNITS * it + UB[n]))
                    for i in range(TPB):
                        for j in range(HG):
                            at_least(pe, m_read, 16 * bx + 4 * i + j)
                            for blk in range(n + 1):
                                width = min(BLK, (4 * n + i + 1) * P - blk * BLK)
                                nc.tensor.matmul(s_ps[:, blk, 0:width], qs[0:ROWS, n, j, i * P:i * P + P],
                                                 ks[0:ROWS, slot, j, blk * BLK:blk * BLK + width], start=True, stop=(blk < n))
                            nc.tensor.matmul(s_ps[:, n, i * P:i * P + P], idb[:], later_t[:], start=False, stop=True).then_inc(m_up, 1)
                    pe.wait_ge(m_read, 16 * bx + 16)
                    if not (isinstance(bx, int) and bx == 0):
                        pe.wait_ge(w_read, W_USES * bx - 2)
                    nc.tensor.transpose(w_ps[0:HG * TPB, 0:P], nmax[:], idf[:]).then_inc(mt_up, 1)
                    pe.wait_ge(m_rows, 16 * bx + 16)

                def scores(it, n, slot, u):
                    unit = UNITS * it + UB[n] + u
                    t0 = max(0, (u - 4 * n) * P)
                    for h in range(2):
                        at_least(pe, probs_ready, 2 * unit + h - 1)
                        for j in (2 * h, 2 * h + 1):
                            last = nc.tensor.matmul(s_ps[:, j, t0:], ks[:, slot, j, u * P:u * P + P], qs[:, n, j, t0:],
                                                    start=True, stop=(u < 4 * n))
                            if u >= 4 * n:
                                last = nc.tensor.matmul(s_ps[:, j, t0:t0 + P], idb[:], later[:], start=False, stop=True)
                        last.then_inc(scores_up, 1)

                def values(it, n, slot, u):
                    unit = UNITS * it + UB[n] + u
                    t0 = max(0, (u - 4 * n) * P)
                    pe.wait_ge(probs_ready, 2 * unit + 2)
                    if u == 0:
                        pe.wait_ge(va_ready, it + 1)
                        at_least(pe, o_read, 4 * it + n - 1)
                    for j in range(HG):
                        last = nc.tensor.matmul(o_ps[n % 2][PAD * j:PAD * (j + 1), t0:], va[:, slot, u, j], pr[:, 2 * (u % 2) + j // 2, j % 2, t0:],
                                                start=(u == 0), stop=(u == 4 * n + 3), tile_position=(0, PAD * j), skip_group_check=True)
                    last.then_inc(pv_done, 1)

                def task(name, bx, n, wn, xn_):
                    if name[0] == "A":
                        c = int(name[1])
                        at_least(pe, w_read, wn)
                        if c == 0:
                            pe.wait_ge(as_in[n % 2], 96 * bx - 96 * (n % 2) + 192)
                        for j in range(HG):
                            last = nc.tensor.matmul(w_ps[:, j * P:j * P + P], kas[:, n % 2, j, c * P:c * P + P],
                                                    qas[:, n % 2, j, c * P:c * P + P], start=True, stop=True)
                        last.then_inc(w_up, 1)
                    elif name in "TZ":
                        src = ot if name == "T" else y2t
                        if name == "T":
                            pe.wait_ge(o_read, bx + 1)
                        else:
                            pe.wait_ge(x_read, xn_)
                        at_least(pe, w_read, wn)
                        for i in range(TPB):
                            last = nc.tensor.transpose(w_ps[:, i * P:i * P + P], src[:, i * P:i * P + P], idf[:])
                        last.then_inc(w_up, 1)
                    elif name == "G":
                        pe.wait_ge(e_ready, bx + 1)
                        pe.wait_ge(lin_in[n % 2], 24 * bx - 24 * (n % 2) + 48)
                        at_least(pe, x_read, xn_)
                        for c in range(TPB):
                            last = nc.tensor.matmul(x_ps[0:CG, c * P:c * P + P], kan[:, n % 2, c], e[:, c].rearrange("p j d -> p (j d)"), start=True, stop=True)
                        last.then_inc(x_up, 1)
                    else:
                        pe.wait_ge(run_ready, 4 * bx + 4)
                        pe.wait_ge(x_read, xn_)
                        for c in range(TPB):
                            nc.tensor.matmul(x_ps[:, c * P:c * P + P], run[:, c], qap[:, n % 2, c * P:c * P + P], start=(c == 0), stop=False, skip_group_check=True)
                            for j in range(HG):
                                last = nc.tensor.matmul(x_ps[PAD * j:PAD * (j + 1), c * P:c * P + P], e[:, c, j], am[:, n % 2, c, j],
                                                        start=False, stop=(c == TPB - 1), tile_position=(0, PAD * j), skip_group_check=True)
                        last.then_inc(x_up, 1)

                def group(it, slot, rnd):
                    pe.wait_ge(ks_in[slot], 96 * rnd + 96)
                    for n in range(NQ):
                        bx = 4 * it + n
                        pe.wait_ge(qs_in[n], 96 * it + 96)
                        with pe.If(slow > 0):
                            maxima(it, n, slot)
                        for u in range(4 * n + 4):
                            scores(it, n, slot, u)
                            if u:
                                values(it, n, slot, u - 1)
                            elif n:
                                values(it, n - 1, slot, 4 * n - 1)
                            elif not (isinstance(it, int) and it == 0):
                                values(it - 1, NQ - 1, 1 - slot, 4 * NQ - 1)
                            for name, wn, xn_ in tasks(it, n, u):
                                if name[0] == "A":
                                    task(name, bx, n, wn, xn_)
                                else:
                                    task(name, bx - 1, (n - 1) % NQ, wn, xn_)

                pe.wait_ge(stacks_ready, 2)
                groups(pe, group)
                values(NG - 1, NQ - 1, 1, 4 * NQ - 1)
                wn, xn_ = W_END, X_END
                for name in LAST:
                    task(name, 4 * NG - 1, NQ - 1, wn, xn_)
                    wn, xn_ = wn + (name in "TZ"), xn_ + (name in "GY")


def finish(nc, cst, z, x, w_proj, w_gate, w_up, w_down, out):
    with ExitStack() as ctx:
        sb = lambda name, shape, dt: ctx.enter_context(nc.sbuf_tensor(name, shape, dt))
        ps = lambda name, shape: ctx.enter_context(nc.psum_tensor(name, shape, F32))
        sem = lambda name: ctx.enter_context(nc.semaphore(name))
        idf = sb("ident_c", [P, P], F32)
        wp = sb("w_proj_sb", [P, KT, C], F32)
        wi = sb("w_int", [P, 3, KT * HID], I32)
        wg = sb("w_gate_sb", [P, KT, HID], F16)
        wu = sb("w_up_sb", [P, KT, HID], F16)
        wd = sb("w_down_sb", [P, NH, C], F32)
        x4 = sb("x_again", [P, TPB, C], F32)
        x1 = sb("x1", [P, NTOK // P, C], F32)
        zs = sb("z_block", [P, TPB, C], F32)
        zt = sb("z_t", [P, KT, BLK], F32)
        a = sb("attended", [P, TPB, C], F32)
        xs = sb("x1n_block", [P, TPB, C], F32)
        xh = sb("x1n_t_hi", [P, KT, BLK], F16)
        xl = sb("x1n_t_lo", [P, KT, BLK], F16)
        sg = sb("silu_gate", [P, 2, BLK], F32)
        h = sb("hidden", [P, NH, BLK], F32)
        f = sb("fed", [P, TPB, C], F32)
        yo = sb("out_block", [P, TPB, C], F32)
        st = [sb(f"st_c{i}", [P, TPB, 6], F32) for i in range(3)]
        mv = [sb(f"mv_c{i}", [P, TPB, 2], F32) for i in range(3)]
        nt = [[sb(f"nt_c{i}{k}", [P, TPB], F32) for k in range(3)] for i in range(3)]
        t_ps = ps("t_ps", [P, KT, BLK])
        a_ps = ps("a_ps", [P, TPB, C])
        g_ps = ps("g_ps", [P, 2, BLK])
        u_ps = ps("up_ps", [P, 2, BLK])

        idle = sem("idle_c")
        fp_in, int_in, w_ready = sem("fp_in"), sem("int_in"), sem("w_ready")
        x_in, z_ready, z_up, zt_ready, a_up, a_ready = sem("x_again_in"), sem("zs_ready"), sem("z_up"), sem("zt_ready"), sem("a_up"), sem("a_ready")
        a_normed, x1_ready, xs_ready, xt_up, hi_ready, lo_ready = sem("a_normed"), sem("x1_ready"), sem("xs_ready"), sem("x1t_up"), sem("x1_hi"), sem("x1_lo")
        gu_up, silu_ready, h_ready, f_up, f_ready, f_normed = sem("gu_up"), sem("silu_ready"), sem("h_ready"), sem("f_up"), sem("f_ready"), sem("f_normed")
        out_ready, stored = sem("out_ready"), sem("out_stored")
        chains = [sem(f"chain_c{i}") for i in range(3)]

        def at_least(engine, s, value):
            if not isinstance(value, int) or value > 0:
                engine.wait_ge(s, value)

        def blocks(engine, body):
            body(0, True)
            with engine.Fori(1, NBLK - 1) as n:
                body(n, True)
            body(NBLK - 1, False)

        def rows(dram, n):
            return dram[ds(n * BLK, BLK), :].rearrange("(i p) c -> p i c", p=P)

        with nc.Block() as block:

            @block.sync
            def _(sp):
                sp.dma_start(x4[:], rows(x, 0)).then_inc(x_in, 16)
                sp.dma_start(idf[:], cst["ident"]).then_inc(fp_in, 16)
                sp.dma_start(wp[:], w_proj.rearrange("(k p) m -> p k m", p=P)).then_inc(fp_in, 16)
                for i, (w, k) in enumerate(((w_gate, KT), (w_up, KT), (w_down, NH))):
                    sp.dma_start(wi[:, i].rearrange("p (k m) -> p k m", k=k), w.rearrange("(k p) m -> p k m", p=P)).then_inc(int_in, 16)

                def store(n):
                    hold(sp, out_ready, n + 1, idle)
                    sp.dma_start(rows(out, n), yo[:]).then_inc(stored, 16)

                def body(n, more):
                    if more:
                        hold(sp, x1_ready, n + 1, idle)
                        sp.dma_start(x4[:], rows(x, n + 1)).then_inc(x_in, 16)
                    if not (isinstance(n, int) and n == 0):
                        store(n - 1)

                blocks(sp, body)
                store(NBLK - 1)
                sp.wait_ge(stored, 16 * NBLK)

            @block.gpsimd
            def _(pool):
                def stage_z(n):
                    hold(pool, z_up, n, idle)
                    for g in range(C // CG):
                        ins = nc.gpsimd.tensor_copy(zs[:, :, g * CG:(g + 1) * CG], z[:, ds((n // NQ * (C // CG) + g) * (T // P) + n % NQ * TPB, TPB), :])
                        ins.then_inc(z_ready, 1)

                def total(n):
                    pool.wait_ge(f_normed, 4 * n + 4)
                    at_least(pool, stored, 16 * n)
                    nc.gpsimd.tensor_tensor(yo[:], f[:], x1[:, ds(n * TPB, TPB), :], ALU.add).then_inc(out_ready, 1)

                def body(n, more):
                    if more:
                        stage_z(n + 1)
                    if not (isinstance(n, int) and n == 0):
                        total(n - 1)

                stage_z(0)
                blocks(pool, body)
                total(NBLK - 1)

            @block.scalar
            def _(act):
                def z_turned(n):
                    act.wait_ge(z_up, n + 1)
                    at_least(act, a_up, n)
                    nc.scalar.copy(zt[:], t_ps[:]).then_inc(zt_ready, 1)

                def attended(n):
                    act.wait_ge(a_up, n + 1)
                    at_least(act, x1_ready, n)
                    nc.scalar.copy(a[:], a_ps[:]).then_inc(a_ready, 1)

                def x_turned(n):
                    act.wait_ge(xt_up, n + 1)
                    at_least(act, gu_up, NH * n)
                    nc.scalar.copy(xh[:], t_ps[:]).then_inc(hi_ready, 1)

                def body(n, more):
                    if more:
                        z_turned(n + 1)
                        attended(n + 1)
                    for m in range(NH):
                        act.wait_ge(gu_up, NH * n + m + 1)
                        at_least(act, h_ready, NH * n + m - 1)
                        nc.scalar.activation(sg[:, m % 2], g_ps[:, m % 2], ACT.Silu, scale=WSCALE).then_inc(silu_ready, 1)
                    if more:
                        x_turned(n + 1)
                    act.wait_ge(f_up, n + 1)
                    at_least(act, out_ready, n)
                    nc.scalar.mul(f[:], g_ps[:].rearrange("p a (i c) -> p (a i) c", c=C), WSCALE).then_inc(f_ready, 1)

                z_turned(0)
                attended(0)
                x_turned(0)
                blocks(act, body)

            @block.vector
            def _(dve):
                dve.wait_ge(int_in, 48)
                nc.vector.tensor_copy(wg[:].rearrange("p k m -> p (k m)"), wi[:, 0]).then_inc(w_ready, 1)
                nc.vector.tensor_copy(wu[:].rearrange("p k m -> p (k m)"), wi[:, 1]).then_inc(w_ready, 1)
                nc.vector.tensor_copy(wd[:].rearrange("p k m -> p (k m)"), wi[:, 2]).then_inc(w_ready, 1)

                def normed(dst, src, which, i):
                    return nc.vector.tensor_scalar(dst, src, mv[which][:, i, 0:1], mv[which][:, i, 1:2], ALU.subtract, ALU.mult)

                def first_norms(n):
                    c1, c2 = Steps(dve, chains[0], LN_STEPS * n), Steps(dve, chains[1], LN_STEPS * n)
                    new = x1[:, ds(n * TPB, TPB), :]

                    def moments1():
                        dve.wait_ge(a_ready, n + 1)
                        ln_moments(nc, c1, [a[:, i, :] for i in range(TPB)], st[0], mv[0], idle)

                    def residual():
                        for i in range(TPB):
                            normed(a[:, i, :], a[:, i, :], 0, i).then_inc(a_normed, 1)
                        dve.wait_ge(a_normed, 4 * n + 4)
                        dve.wait_ge(x_in, 16 * n + 16)
                        nc.vector.tensor_tensor(new, x4[:], a[:], ALU.add).then_inc(x1_ready, 1)

                    def moments2():
                        hold(dve, x1_ready, n + 1, idle)
                        ln_moments(nc, c2, [x1[:, ds(n * TPB + i, 1), :].rearrange("p a c -> p (a c)") for i in range(TPB)], st[1], mv[1], idle)

                    def norm2():
                        at_least(dve, xt_up, n)
                        for i in range(TPB):
                            normed(xs[:, i, :], x1[:, ds(n * TPB + i, 1), :].rearrange("p a c -> p (a c)"), 1, i).then_inc(xs_ready, 1)

                    return [moments1, lambda: ln_rsqrt(nc, c1, mv[0], nt[0]), residual,
                            moments2, lambda: ln_rsqrt(nc, c2, mv[1], nt[1]), norm2]

                def low_part(n):
                    dve.wait_ge(hi_ready, n + 1)
                    at_least(dve, gu_up, NH * n)
                    nc.vector.tensor_tensor(xl[:], t_ps[:], xh[:], ALU.subtract).then_inc(lo_ready, 1)

                def last_norm(n):
                    dve.wait_ge(f_ready, n + 1)
                    chain = Steps(dve, chains[2], LN_STEPS * n)
                    ln_moments(nc, chain, [f[:, i, :] for i in range(TPB)], st[2], mv[2], idle)
                    ln_rsqrt(nc, chain, mv[2], nt[2])
                    for i in range(TPB):
                        normed(f[:, i, :], f[:, i, :], 2, i).then_inc(f_normed, 1)

                def body(n, more):
                    pieces = first_norms(n + 1) if more else []
                    for m in range(NH):
                        dve.wait_ge(silu_ready, NH * n + m + 1)
                        at_least(dve, f_up, n)
                        nc.vector.scalar_tensor_tensor(h[:, m], u_ps[:, m % 2], WSCALE, sg[:, m % 2], ALU.mult, ALU.mult).then_inc(h_ready, 1)
                        if more:
                            pieces[m]()
                    if more:
                        low_part(n + 1)
                    if not (isinstance(n, int) and n == 0):
                        last_norm(n - 1)

                for piece in first_norms(0):
                    piece()
                low_part(0)
                blocks(dve, body)
                last_norm(NBLK - 1)

            @block.tensor
            def _(pe):
                def project_z(n):
                    pe.wait_ge(z_ready, 4 * n + 4)
                    at_least(pe, lo_ready, n)
                    for i in range(TPB):
                        for k in range(KT):
                            last = nc.tensor.transpose(t_ps[:, k, i * P:i * P + P], zs[:, i, k * P:k * P + P], idf[:])
                    last.then_inc(z_up, 1)
                    pe.wait_ge(zt_ready, n + 1)
                    at_least(pe, a_ready, n)
                    for i in range(TPB):
                        for k in range(KT):
                            last = nc.tensor.matmul(a_ps[:, i], zt[:, k, i * P:i * P + P], wp[:, k], start=(k == 0), stop=(k == KT - 1))
                    last.then_inc(a_up, 1)

                def turn_x(n):
                    pe.wait_ge(xs_ready, 4 * n + 4)
                    for i in range(TPB):
                        for k in range(KT):
                            last = nc.tensor.transpose(t_ps[:, k, i * P:i * P + P], xs[:, i, k * P:k * P + P], idf[:])
                    last.then_inc(xt_up, 1)

                def body(n, more):
                    if more:
                        project_z(n + 1)
                    pe.wait_ge(lo_ready, n + 1)
                    for m in range(NH):
                        at_least(pe, h_ready, NH * n + m - 1)
                        if m < 2:
                            at_least(pe, f_ready, n)
                        for w, bank in ((wg, g_ps), (wu, u_ps)):
                            for k in range(KT):
                                for part in (xh, xl):
                                    last = nc.tensor.matmul(bank[:, m % 2], w[:, k, m * P:m * P + P], part[:, k],
                                                            start=(k == 0 and part is xh), stop=(k == KT - 1 and part is xl))
                        last.then_inc(gu_up, 1)
                    if more:
                        turn_x(n + 1)
                    pe.wait_ge(h_ready, NH * n + NH)
                    for i in range(TPB):
                        for k in range(NH):
                            last = nc.tensor.matmul(g_ps[:, i // 2, i % 2 * C:i % 2 * C + C], h[:, k, i * P:i * P + P], wd[:, k],
                                                    start=(k == 0), stop=(k == NH - 1))
                    last.then_inc(f_up, 1)

                pe.wait_ge(fp_in, 32)
                project_z(0)
                turn_x(0)
                pe.wait_ge(w_ready, 3)
                blocks(pe, body)


def layer(nc, t):
    parts = nc.dram_tensor("parts_dram", (4, 3, B * C, T), BF16, kind="Internal").ap()
    qa32 = nc.dram_tensor("qa32_dram", (B * C, T), F32, kind="Internal").ap()
    ka_nat = nc.dram_tensor("ka_nat_dram", (NG * T, CG), F32, kind="Internal").ap()
    xn_dram = nc.dram_tensor("xn_dram", (NG * T + 1, CG), F32, kind="Internal").ap()
    rows_dram = nc.dram_tensor("minus_max_dram", (NM, HG * BLK), BF16, kind="Internal").ap()
    with nc.sbuf_tensor("flag", [1, 1], I32) as flag, nc.sbuf_tensor("z", [P, NG * T // P, CG], F32) as z:
        project(nc, t["x"], t["w_attn"], t["w_k2"], t["ident"], t["heads"], flag, parts, qa32, ka_nat, xn_dram)
        attend(nc, t, flag, z, parts, qa32, ka_nat, xn_dram, rows_dram)
        finish(nc, t, z, t["x"], t["w_proj"], t["w_gate"], t["w_up"], t["w_down"], t["out"])


def kernel(**inputs):
    import ml_dtypes
    import numpy as np
    import concourse.bacc as bacc
    from concourse.bass_utils import run_bass_kernel_spmd

    bf16 = ml_dtypes.bfloat16
    i = np.arange(P)
    own = np.zeros((CG, P), np.float32)
    for j in range(HG):
        own[j * D:(j + 1) * D, j * PAD:j * PAD + D] = 1
    arrays = {
        "x": np.ascontiguousarray(inputs["L0_attn_x"]).reshape(NTOK, C),
        "w_attn": np.ascontiguousarray(inputs["L0_attn_W_attn"]),
        "w_k2": np.ascontiguousarray(inputs["L0_attn_W_k2"]),
        "w_proj": np.ascontiguousarray(inputs["L0_attn_W_proj"]),
        "w_gate": np.ascontiguousarray(np.asarray(inputs["L0_ffn_w_gate"]).T),
        "w_up": np.ascontiguousarray(np.asarray(inputs["L0_ffn_w_up"]).T),
        "w_down": np.ascontiguousarray(np.asarray(inputs["L0_ffn_w_down"]).T),
        "ident": np.eye(P, dtype=np.float32),
        "ident_bf": np.eye(P).astype(bf16),
        "heads": np.repeat(np.eye(P // D, dtype=np.float32), D, axis=0),
        "later": np.where(i[:, None] > i[None, :], NEG, 0.0).astype(bf16),
        "later_t": np.where(i[:, None] < i[None, :], NEG, 0.0).astype(bf16),
        "before": (i[:, None] < i[None, :]).astype(np.float32),
        "own": own,
    }
    nc = bacc.Bacc("TRN2", target_bir_lowering=False, num_devices=1)
    t = {name: nc.dram_tensor(f"in_{name}", a.shape, mybir.dt.from_np(a.dtype), kind="ExternalInput").ap()
         for name, a in arrays.items()}
    t["out"] = nc.dram_tensor("out", (NTOK, C), F32, kind="ExternalOutput").ap()
    layer(nc, t)
    r = run_bass_kernel_spmd(nc, [{f"in_{name}": a for name, a in arrays.items()}], core_ids=[0])
    return r.results[0]["out"].reshape(B, T, C)
```

```python
from contextlib import ExitStack

import concourse.bass as bass
from concourse import mybir

P = 128
BLK = 512
TPB = BLK // P
B, T, C = 2, 2048, 256
NTOK = B * T
NBLK = NTOK // BLK
NQ = T // BLK
H, D = 16, 16
HG = 4
CG = HG * D
HID = 768
NH = HID // P
KT = C // P
PAD = 32
TERMS = ((0, 0), (0, 1), (1, 0), (0, 2), (2, 0), (1, 1))
ROWS = D * len(TERMS)
NM = 3
SCALE = 1.0 / D ** 0.5
MA_SCALE = 0.02 * SCALE
LEAK = 0.02 * SCALE
WSCALE = 1.0 / 127.0
EPS = 1e-5
SAFE = 75.0
NEG = -1e30

ALU = mybir.AluOpType
ACT = mybir.ActivationFunctionType
F32, BF16, F16, I32 = mybir.dt.float32, mybir.dt.bfloat16, mybir.dt.float16, mybir.dt.int32
AX = mybir.AxisListType
ds = bass.ds


def hold(engine, sem, value, idle):
    if not isinstance(value, int) or value > 0:
        engine.wait_ge(sem, value)
        engine.sem_inc(idle, 1)


class Steps:

    def __init__(self, engine, sem, base=0):
        self.engine, self.sem, self.base, self.n = engine, sem, base, 0

    def link(self, ins, idle=None):
        self.n += 1
        ins.then_inc(self.sem, 1)
        if idle is None:
            self.engine.wait_ge(self.sem, self.base + self.n)
        else:
            hold(self.engine, self.sem, self.base + self.n, idle)


LN_STEPS = 14


def ln_moments(nc, chain, rows, st, mv, idle):
    for i, row in enumerate(rows):
        ins = nc.vector.bn_stats(st[:, i, :], row)
    chain.link(ins, idle)
    for i in range(len(rows)):
        ins = nc.vector.bn_aggr(mv[:, i, :], st[:, i, :])
    chain.link(ins)


def ln_rsqrt(nc, chain, mv, nt):
    v, y, t = nt
    chain.link(nc.vector.tensor_scalar(v[:], mv[:, :, 1], EPS, None, ALU.add))
    chain.link(nc.vector.tensor_scalar(t[:].bitcast(I32), v[:].bitcast(I32), 1, None, ALU.logical_shift_right))
    chain.link(nc.vector.tensor_scalar(y[:].bitcast(I32), t[:].bitcast(I32), -1.0, float(0x5F3759DF), ALU.mult, ALU.add))
    for k in range(3):
        chain.link(nc.vector.tensor_tensor(t[:], y[:], y[:], ALU.mult))
        chain.link(nc.vector.scalar_tensor_tensor(t[:], t[:], -0.5, v[:], ALU.mult, ALU.mult))
        out = y[:] if k < 2 else mv[:, :, 1]
        chain.link(nc.vector.scalar_tensor_tensor(out, t[:], 1.5, y[:], ALU.add, ALU.mult))


def project(nc, x, w_qk, w_k2, ident, heads, flag, parts, qa32, ka_nat, xn_dram):
    Q, K, KA, QA = 0, 2, 4, 6
    with ExitStack() as ctx:
        sb = lambda name, shape, dt: ctx.enter_context(nc.sbuf_tensor(name, shape, dt))
        ps = lambda name, shape: ctx.enter_context(nc.psum_tensor(name, shape, F32))
        sem = lambda name: ctx.enter_context(nc.semaphore(name))
        w = sb("w_all", [P, KT, 3 * C], F32)
        idf = sb("ident_a", [P, P], F32)
        ind = sb("head_of_channel", [P, P // D], F32)
        x4 = sb("x_block", [P, TPB, C], F32)
        xs = sb("xn_block", [P, TPB, C], F32)
        xt = sb("xn_t", [P, KT, BLK], F32)
        hi_lo = sb("parts_sb", [P, 8, 3, BLK], BF16)
        rest = sb("rest", [P, 8, BLK], F32)
        small = sb("q_leak", [P, 2, BLK], F32)
        qaf = sb("qa_f32", [P, 2, BLK], F32)
        kaf = sb("ka_f32", [P, 2, BLK], F32)
        kn = sb("ka_nat_sb", [P, TPB, C], F32)
        zrow = sb("zero_row", [1, CG], F32)
        st = sb("st_a", [P, TPB, 6], F32)
        mv = sb("mv_a", [P, TPB, 2], F32)
        nt = [sb(f"nt_a{i}", [P, TPB], F32) for i in range(3)]
        peak = sb("peak", [P, 8, BLK], BF16)
        top = sb("peak_top", [P, 8], F32)
        prod = sb("peak_prod", [P, 2], F32)
        bound = sb("bound", [1, 1], F32)
        xt_ps = ps("xt_ps", [P, KT, BLK])
        u = ps("u_ps", [P, 4, BLK])
        kn_ps = ps("kn_ps", [P, TPB, C])

        idle = sem("idle_a")
        w_in, x_in, xn_done, xt_up, xt_down = sem("w_in"), sem("x_in"), sem("xn_done"), sem("xt_up"), sem("xt_down")
        u_ready, u_read = sem("u_ready"), sem("u_read")
        hi_ready, leak_ready, kaf_ready, qaf_ready = sem("hi_ready"), sem("leak_ready"), sem("kaf_ready"), sem("qaf_ready")
        rest_ready, mid_dve, mid_act, lo_ready = sem("rest_ready"), sem("mid_dve"), sem("mid_act"), sem("lo_ready")
        kn_up, kn_down = sem("kn_up"), sem("kn_down")
        stored = [sem(f"stored{s}") for s in range(8)]
        qa_stored, kn_stored, xn_stored, z_stored = [sem("qa_stored0"), sem("qa_stored1")], sem("kn_stored"), sem("xn_stored"), sem("z_stored")
        chain_s, peak_done, prod_ready, sum_ready, z_ready, bound_ready = sem("chain_a"), sem("peak_done"), sem("prod_ready"), sem("sum_ready"), sem("z_ready"), sem("bound_ready")

        def tokens(dram, n, g):
            return dram[ds((n // NQ * (C // CG) + g) * T + n % NQ * BLK, BLK), :].rearrange("(i p) c -> p i c", p=P)

        def load_x(sp, n):
            sp.dma_start(x4[:], x[ds(n * BLK, BLK), :].rearrange("(i p) c -> p i c", p=P)).then_inc(x_in, 16)

        with nc.Block() as block:

            @block.sync
            def _(sp):
                load_x(sp, 0)
                sp.dma_start(idf[:], ident).then_inc(w_in, 16)
                sp.dma_start(w[:, :, 0:2 * C], w_qk.rearrange("(k p) m -> p k m", p=P)).then_inc(w_in, 16)
                sp.dma_start(w[:, :, 2 * C:], w_k2.rearrange("(k p) m -> p k m", p=P)).then_inc(w_in, 16)
                sp.dma_start(ind[:], heads).then_inc(w_in, 16)
                sp.wait_ge(z_ready, 1)
                sp.dma_start(xn_dram[NTOK * C // CG:, :], zrow[:]).then_inc(z_stored, 16)
                for s in stored + qa_stored:
                    sp.sem_inc(s, 16)
                sp.sem_inc(kn_stored, 64)

                def body(n, more):
                    if more:
                        hold(sp, xn_done, 4 * n + 4, idle)
                        load_x(sp, n + 1)
                    hold(sp, xn_done, 4 * n + 4, idle)
                    for g in range(C // CG):
                        sp.dma_start(tokens(xn_dram, n, g), xs[:, :, g * CG:(g + 1) * CG]).then_inc(xn_stored, 16)
                    for s in range(8):
                        hold(sp, lo_ready, 8 * n + s + 1, idle)
                        sp.dma_start(parts[s // 2, :, ds(n // NQ * C + s % 2 * P, P), ds(n % NQ * BLK, BLK)].rearrange("a p t -> p a t"),
                                     hi_lo[:, s]).then_inc(stored[s], 16)
                        if s == 1:
                            for c in range(2):
                                hold(sp, qaf_ready, 2 * n + c + 1, idle)
                                sp.dma_start(qa32[ds(n // NQ * C + c * P, P), ds(n % NQ * BLK, BLK)], qaf[:, c]).then_inc(qa_stored[c], 16)
                    hold(sp, kn_down, n + 2, idle)
                    for g in range(C // CG):
                        sp.dma_start(tokens(ka_nat, n, g), kn[:, :, g * CG:(g + 1) * CG]).then_inc(kn_stored, 16)

                with sp.Fori(0, NBLK - 1) as n:
                    body(n, True)
                body(NBLK - 1, False)
                for s in stored + qa_stored:
                    sp.wait_ge(s, 16 * NBLK + 16)
                sp.wait_ge(kn_stored, 64 * NBLK + 64)
                sp.wait_ge(xn_stored, 64 * NBLK)
                sp.wait_ge(z_stored, 16)

            @block.vector
            def _(dve):
                nc.vector.memset(zrow[:], 0.0).then_inc(z_ready, 1)
                nc.vector.memset(peak[:], 0.0).then_inc(peak_done, 1)
                dve.sem_inc(u_read, 4)
                dve.sem_inc(rest_ready, 8)

                def norm(n):
                    dve.wait_ge(x_in, 16 * n + 16)
                    chain = Steps(dve, chain_s, n * LN_STEPS)
                    ln_moments(nc, chain, [x4[:, i, :] for i in range(TPB)], st, mv, idle)
                    ln_rsqrt(nc, chain, mv, nt)
                    assert chain.n == LN_STEPS
                    if not (isinstance(n, int) and n == 0):
                        dve.wait_ge(xt_up, n)
                        dve.wait_ge(xn_stored, 64 * n)
                    for i in range(TPB):
                        nc.vector.tensor_scalar(xs[:, i, :], x4[:, i, :],
                                                mv[:, i, 0:1], mv[:, i, 1:2], ALU.subtract, ALU.mult).then_inc(xn_done, 1)

                def mid(n, s):
                    dve.wait_ge(rest_ready, 8 * n + 8 + s + 1)
                    nc.vector.tensor_copy(hi_lo[:, s, 1], rest[:, s]).then_inc(mid_dve, 1)

                def body(n, more):
                    for s in range(4):
                        dve.wait_ge(hi_ready, 8 * n + s + 1)
                        if s < 2:
                            dve.wait_ge(leak_ready, 2 * n + s + 1)
                        nc.vector.tensor_tensor(rest[:, s], u[:, s], hi_lo[:, s, 0], ALU.subtract).then_inc(rest_ready, 1)
                        if s < 2:
                            dve.wait_ge(qa_stored[s], 16 * n + 16)
                            dve.wait_ge(rest_ready, 8 * n + 7 + s)
                            nc.vector.scalar_tensor_tensor(qaf[:, s], u[:, s], SCALE, small[:, s], ALU.mult, ALU.min).then_inc(qaf_ready, 1)
                        dve.wait_ge(peak_done, 4 * n + s + 1)
                        nc.vector.tensor_tensor(peak[:, s], hi_lo[:, s, 0], peak[:, s], ALU.max)
                        nc.vector.tensor_tensor(peak[:, 4 + s], hi_lo[:, s, 0], peak[:, 4 + s], ALU.min).then_inc(peak_done, 1)
                        if s % 2 == 0:
                            mid(n, s)
                    if more:
                        norm(n + 1)
                    for s in range(4, 8):
                        dve.wait_ge(hi_ready, 8 * n + s + 1)
                        f = kaf[:, s - 4] if s < 6 else qaf[:, s - 6]
                        nc.vector.tensor_tensor(rest[:, s], f, hi_lo[:, s, 0], ALU.subtract).then_inc(rest_ready, 1)
                        if s % 2 == 0:
                            mid(n, s)

                norm(0)
                with dve.Fori(0, NBLK - 1) as n:
                    body(n, True)
                body(NBLK - 1, False)
                dve.wait_ge(peak_done, 4 * NBLK + 1)
                nc.vector.tensor_reduce(top[:, 0:4], peak[:, 0:4], AX.X, ALU.max)
                nc.vector.tensor_reduce(top[:, 4:8], peak[:, 4:8], AX.X, ALU.min).then_inc(peak_done, 1)
                dve.wait_ge(peak_done, 4 * NBLK + 2)
                nc.vector.scalar_tensor_tensor(top[:, 0:4], top[:, 4:8], -1.0, top[:, 0:4], ALU.mult, ALU.max).then_inc(prod_ready, 1)
                dve.wait_ge(prod_ready, 1)
                nc.vector.tensor_tensor(prod[:], top[:, 0:2], top[:, 2:4], ALU.mult).then_inc(prod_ready, 1)
                dve.wait_ge(sum_ready, 1)
                nc.vector.tensor_reduce(bound[:], kn_ps[0:1, 0, 0:KT * P // D], AX.X, ALU.max).then_inc(bound_ready, 1)
                dve.wait_ge(bound_ready, 1)
                nc.vector.tensor_scalar(flag[:], bound[:], SCALE * 1.01, SAFE, ALU.mult, ALU.is_gt).then_inc(bound_ready, 1)

            @block.scalar
            def _(act):
                act.sem_inc(kaf_ready, 2)
                act.sem_inc(kn_down, 1)

                def xt_evac(n):
                    act.wait_ge(xt_up, n + 1)
                    act.wait_ge(u_ready, 6 * n + 1)
                    nc.scalar.copy(xt[:], xt_ps[:]).then_inc(xt_down, 1)

                def hi(n, s, src):
                    act.wait_ge(stored[s], 16 * n + 16)
                    nc.scalar.copy(hi_lo[:, s, 0], src).then_inc(hi_ready, 1)

                def mid(n, s):
                    act.wait_ge(rest_ready, 8 * n + 8 + s + 1)
                    nc.scalar.copy(hi_lo[:, s, 1], rest[:, s]).then_inc(mid_act, 1)

                def body(n, more):
                    for s in range(4):
                        act.wait_ge(u_ready, 6 * n + s + 2)
                        hi(n, s, u[:, s])
                        if s < 2:
                            nc.scalar.mul(small[:, s], u[:, s], LEAK).then_inc(leak_ready, 1)
                        if s == 3:
                            mid(n, 1)
                    for s in range(2):
                        act.wait_ge(u_ready, 6 * n + s + 6)
                        act.wait_ge(rest_ready, 8 * n + s + 5)
                        nc.scalar.activation(kaf[:, s], u[:, s], ACT.Sigmoid, scale=MA_SCALE).then_inc(kaf_ready, 1)
                    if more:
                        xt_evac(n + 1)
                    mid(n, 3)
                    act.wait_ge(kaf_ready, 2 * n + 4)
                    for s in range(4, 6):
                        hi(n, s, kaf[:, s - 4])
                    for s in range(6, 8):
                        act.wait_ge(qaf_ready, 2 * n + s - 5)
                        hi(n, s, qaf[:, s - 6])
                    mid(n, 5)
                    mid(n, 7)
                    act.wait_ge(kn_up, n + 1)
                    act.wait_ge(kn_stored, 64 * n + 64)
                    nc.scalar.copy(kn[:], kn_ps[:]).then_inc(kn_down, 1)

                xt_evac(0)
                with act.Fori(0, NBLK - 1) as n:
                    body(n, True)
                body(NBLK - 1, False)

            @block.gpsimd
            def _(pool):
                def body(n):
                    for s in range(8):
                        pool.wait_ge(mid_dve if s % 2 == 0 else mid_act, 4 * n + s // 2 + 1)
                        nc.gpsimd.tensor_tensor(hi_lo[:, s, 2], rest[:, s], hi_lo[:, s, 1], ALU.subtract).then_inc(lo_ready, 1)

                with pool.Fori(0, NBLK) as n:
                    body(n)

            @block.tensor
            def _(pe):
                pe.sem_inc(u_ready, 1)

                def turn_x(n):
                    pe.wait_ge(xn_done, 4 * n + 4)
                    if not (isinstance(n, int) and n == 0):
                        pe.wait_ge(xt_down, n)
                    for i in range(TPB):
                        for k in range(KT):
                            last = nc.tensor.transpose(xt_ps[:, k, i * P:i * P + P], xs[:, i, k * P:k * P + P], idf[:])
                    last.then_inc(xt_up, 1)

                def tile(n, m):
                    if m == 0:
                        pe.wait_ge(kaf_ready, 2 * n + 1)
                    elif m == 1:
                        pe.wait_ge(kaf_ready, 2 * n + 2)
                    elif m < 4:
                        pe.wait_ge(rest_ready, 8 * n + m + 1)
                    else:
                        pe.wait_ge(qaf_ready, 2 * n + m - 3)
                    for k in range(KT):
                        ins = nc.tensor.matmul(u[:, m % 4], w[:, k, m * P:m * P + P], xt[:, k], start=(k == 0), stop=(k == KT - 1))
                    ins.then_inc(u_ready, 1)

                def body(n, more):
                    pe.wait_ge(xt_down, n + 1)
                    for m in range(6):
                        tile(n, m)
                    if more:
                        turn_x(n + 1)
                    pe.wait_ge(kaf_ready, 2 * n + 4)
                    pe.wait_ge(kn_down, n + 1)
                    for i in range(TPB):
                        for k in range(KT):
                            last = nc.tensor.transpose(kn_ps[:, i, k * P:k * P + P], kaf[:, k, i * P:i * P + P], idf[:])
                    last.then_inc(kn_up, 1)

                pe.wait_ge(w_in, 64)
                turn_x(0)
                with pe.Fori(0, NBLK - 1) as n:
                    body(n, True)
                body(NBLK - 1, False)
                pe.wait_ge(prod_ready, 2)
                pe.wait_ge(kn_down, NBLK + 1)
                for k in range(KT):
                    last = nc.tensor.matmul(kn_ps[0:1, 0, k * (P // D):(k + 1) * (P // D)], prod[:, k:k + 1], ind[:], start=True, stop=True)
                last.then_inc(sum_ready, 1)


NG = B * C // CG
UB = [4 * n * (n + 1) // 2 for n in range(NQ + 1)]
UNITS = UB[NQ]
PRING = 4
LAG = 2
SCHEDULE = [(0, "A0", 0), (1, "A1", 0), (2, "T", -1), (3, "A2", 0), (4, "G", -1), (5, "A3", 0), (6, "Y", -1), (7, "Z", -1),
            (8, "T", 0), (9, "A0", 1), (10, "G", 0), (11, "Y", 0), (12, "A1", 1), (13, "Z", 0),
            (14, "T", 1), (15, "A2", 1), (16, "G", 1), (17, "A3", 1), (18, "Y", 1), (19, "Z", 1),
            (20, "A0", 2), (21, "A1", 2), (22, "A2", 2), (23, "A3", 2),
            (26, "T", 2), (27, "A0", 3), (28, "G", 2), (29, "A1", 3), (30, "Y", 2), (31, "Z", 2), (33, "A2", 3), (35, "A3", 3)]
LAST = "TGYZ"
W_STEPS = [step[1:] for step in SCHEDULE if step[1] not in ("G", "Y")]
X_STEPS = [step[1:] for step in SCHEDULE if step[1] in ("G", "Y")]


def used(steps, it, upto):
    if isinstance(it, int) and it == 0:
        return sum(m >= 0 for _, m in steps[:upto])
    return len(steps) * it + upto - sum(m < 0 for _, m in steps)


def used_with(steps, it, name, m):
    return used(steps, it, steps.index((name, m)) + 1)


def attend(nc, cst, flag, z, parts, qa32, ka_nat, xn_dram, rows_dram):
    with ExitStack() as ctx:
        sb = lambda name, shape, dt: ctx.enter_context(nc.sbuf_tensor(name, shape, dt))
        ps = lambda name, shape: ctx.enter_context(nc.psum_tensor(name, shape, F32))
        sem = lambda name: ctx.enter_context(nc.semaphore(name))
        idf = sb("ident_f", [P, P], F32)
        idb = sb("ident_b", [P, P], BF16)
        causal = sb("causal", [P, P], F32)
        later_t = sb("later_keys_t", [P, P], BF16)
        before = sb("before", [P, P], F32)
        own = sb("own_head", [CG, P], F32)
        ks = sb("k_stack", [ROWS + NM, 2, HG, T], BF16)
        qs = sb("q_stack", [ROWS + NM, NQ, HG, BLK], BF16)
        kas = sb("ka_stack", [ROWS, 2, HG, BLK], BF16)
        qas = sb("qa_stack", [ROWS, 2, HG, BLK], BF16)
        qap = sb("qa_plain", [CG, 2, BLK], F32)
        kan = sb("ka_tokens", [P, 2, TPB, CG], F32)
        vnext = sb("v_next", [P, 2, TPB, CG], F32)
        vraw = sb("v_raw", [P, T // P, CG], F32)
        va = sb("v_and_one", [P, 2, T // P, HG, PAD], F32)
        pr = sb("probs", [P, PRING, 2, 2, BLK], F32)
        am = sb("local_products", [P, 2, TPB, HG, P], F32)
        e = sb("e_padded", [P, TPB, HG, PAD], F32)
        ot = sb("y_t", [P, BLK], F32)
        y2t = sb("y2_t", [P, BLK], F32)
        inv = sb("inv_sum", [P, TPB, HG], F32)
        y = sb("y_tokens", [P, TPB, HG, D], F32)
        run = sb("running", [CG, TPB + 1, P], F32)
        gm = sb("ka_e", [CG, TPB, P], F32)
        nmax = sb("minus_max", [P, HG * TPB], F32)
        nsplit = sb("minus_max_rest", [HG * TPB, P], F32)
        nrow = sb("minus_max_parts", [HG * TPB, NM, P], BF16)
        s_ps = ps("s_ps", [P, 4, BLK])
        o_ps = [ps(f"o_ps{i}", [P, BLK]) for i in range(2)]
        w_ps = ps("w_ps", [P, BLK])
        x_ps = ps("x_ps", [P, BLK])

        idle = sem("idle_b")
        consts_in, pads_ready, stacks_ready = sem("consts_in"), sem("pads_ready"), sem("stacks_ready")
        ks_in = [sem(f"ks_in{i}") for i in range(2)]
        qs_in = [sem(f"qs_in{i}") for i in range(NQ)]
        as_in = [sem(f"as_in{i}") for i in range(2)]
        lin_in = [sem(f"lin_in{i}") for i in range(2)]
        v_in, va_ready = sem("v_in"), sem("va_ready")
        scores_up, probs_ready, pv_done, o_read = sem("scores_up"), sem("probs_ready"), sem("pv_done"), sem("o_read")
        w_up, w_read, x_up, x_read = sem("w_up"), sem("w_read"), sem("x_up"), sem("x_read")
        masked, e_ready, run_ready, chain_s = sem("masked"), sem("e_ready"), sem("run_ready"), sem("chain_b")
        m_up, m_read, mt_up, mt_parts, m_out, m_rows, m_chain, clamped = sem("m_up"), sem("m_read"), sem("mt_up"), sem("mt_parts"), sem("m_out"), sem("m_rows"), sem("m_chain"), sem("clamped")

        def at_least(engine, s, value):
            if not isinstance(value, int) or value > 0:
                engine.wait_ge(s, value)

        def groups(engine, group):
            group(0, 0, 0)
            with engine.Fori(0, (NG - 2) // 2) as i:
                group(2 * i + 1, 1, i)
                group(2 * i + 2, 0, i + 1)
            group(NG - 1, 1, (NG - 1) // 2)

        def tasks(it, at):
            first = isinstance(it, int) and it == 0
            for unit, name, m in SCHEDULE:
                if unit == at and not (first and m < 0):
                    before_w = used(W_STEPS, it, sum(st[0] < at for st in SCHEDULE if st[1] not in ("G", "Y")))
                    before_x = used(X_STEPS, it, sum(st[0] < at for st in SCHEDULE if st[1] in ("G", "Y")))
                    yield name, 4 * it + m, m % NQ, before_w, before_x

        W_END, X_END = used(W_STEPS, NG, 0), used(X_STEPS, NG, 0)

        with nc.Block() as block:

            @block.sync
            def _(sp):
                for dst, name in ((idf, "ident"), (idb, "ident_bf"), (causal, "causal"), (later_t, "later_t"), (before, "before"), (own, "own")):
                    sp.dma_start(dst[:], cst[name]).then_inc(consts_in, 16)

                def stack(dst, kind, side, it, cols, s):
                    for r, term in enumerate(TERMS):
                        sp.dma_start(dst[r * D:(r + 1) * D],
                                     parts[kind, term[side], ds(it * CG, CG), cols].rearrange("(j d) t -> d j t", d=D)).then_inc(s, 16)

                def group(it, slot, rnd):
                    hold(sp, pv_done, UNITS * it - UNITS + 1, idle)
                    stack(ks[:, slot], 1, 0, it, slice(0, T), ks_in[slot])
                    hold(sp, va_ready, it, idle)
                    sp.dma_start(vraw[:], xn_dram[ds(it * T, T), :].rearrange("(i p) c -> p i c", p=P)).then_inc(v_in, 16)
                    for n in range(NQ):
                        bx = 4 * it + n
                        cols = slice(n * BLK, n * BLK + BLK)
                        hold(sp, pv_done, UNITS * it - UNITS + UB[n + 1], idle)
                        stack(qs[:, n], 0, 1, it, cols, qs_in[n])
                        if not (isinstance(it, int) and it == 0 and n < 2):
                            other = (it, n - 2) if n >= 2 else (it - 1, n + 2)
                            hold(sp, w_read, used_with(W_STEPS, other[0], "A3", other[1]), idle)
                        stack(kas[:, n % 2], 2, 0, it, cols, as_in[n % 2])
                        stack(qas[:, n % 2], 3, 1, it, cols, as_in[n % 2])
                        if not (isinstance(it, int) and it == 0 and n < 2):
                            y_at = {0: (it - 1, 2), 1: (it, -1), 2: (it, 0), 3: (it, 1)}[n]
                            hold(sp, x_read, used_with(X_STEPS, y_at[0], "Y", y_at[1]), idle)
                        sp.dma_start(qap[:, n % 2], qa32[ds(it * CG, CG), cols]).then_inc(lin_in[n % 2], 16)
                        sp.dma_start(kan[:, n % 2], ka_nat[ds(it * T + n * BLK, BLK), :].rearrange("(i p) c -> p i c", p=P)).then_inc(lin_in[n % 2], 16)
                        sp.dma_start(vnext[:, n % 2], xn_dram[ds(it * T + n * BLK + 1, BLK), :].rearrange("(i p) c -> p i c", p=P)).then_inc(lin_in[n % 2], 16)

                groups(sp, group)

            @block.gpsimd
            def _(pool):
                nc.gpsimd.memset(va[:], 0.0).then_inc(pads_ready, 1)
                nc.gpsimd.memset(e[:], 0.0).then_inc(pads_ready, 1)
                pool.wait_ge(pads_ready, 1)
                for slot in range(2):
                    nc.gpsimd.memset(va[:, slot, :, :, D:D + 1], 1.0).then_inc(pads_ready, 1)

                def values(it, slot):
                    pool.wait_ge(v_in, 16 * it + 16)
                    hold(pool, pv_done, UNITS * it - UNITS, idle)
                    nc.gpsimd.tensor_copy(va[:, slot, :, :, 0:D], vraw[:].rearrange("p i (j d) -> p i j d", d=D)).then_inc(va_ready, 1)

                def next_minus_y(bx, n, w_use):
                    pool.wait_ge(w_read, w_use + 1)
                    pool.wait_ge(lin_in[n % 2], 24 * bx - 24 * (n % 2) + 48)
                    nc.gpsimd.tensor_tensor(e[:, :, :, 0:D], vnext[:, n % 2].rearrange("p i (j d) -> p i j d", d=D), y[:], ALU.subtract).then_inc(e_ready, 1)

                def group(it, slot, rnd):
                    for at in range(UNITS):
                        for name, bx, n, wn, xn_ in tasks(it, at):
                            if name == "T":
                                next_minus_y(bx, n, wn)
                            if name == "T" and n == 2 and not (isinstance(it, int) and it == NG - 1):
                                values(it + 1, 1 - slot)

                values(0, 0)
                groups(pool, group)
                next_minus_y(4 * NG - 1, NQ - 1, W_END)

            @block.scalar
            def _(act):
                slow = act.value_load(flag[0:1, 0:1], min_val=0, max_val=1)

                def exp(it, n, u, clamp):
                    unit = UNITS * it + UB[n] + u
                    t0 = max(0, (u - 4 * n) * P)
                    for h in range(2):
                        act.wait_ge(scores_up, 2 * unit + h + 1)
                        if clamp:
                            tile = s_ps[:, 2 * h:2 * h + 2, t0:t0 + P]
                            done = 4 * (4 * (4 * it + n) + u - 4 * n) + 2 * h
                            nc.scalar.activation(tile, tile, ACT.Relu, scale=-1.0).then_inc(clamped, 1)
                            act.wait_ge(clamped, done + 1)
                            nc.scalar.mul(tile, tile, -1.0).then_inc(clamped, 1)
                            act.wait_ge(clamped, done + 2)
                        at_least(act, pv_done, unit - PRING + 1)
                        nc.scalar.activation(pr[:, u % PRING, h, :, t0:], s_ps[:, 2 * h:2 * h + 2, t0:], ACT.Exp, scale=SCALE).then_inc(probs_ready, 1)

                def group(it, slot, rnd):
                    for n in range(NQ):
                        with act.If(slow > 0):
                            act.wait_ge(mt_parts, 12 * it + 3 * n + 3)
                            act.dma_start(rows_dram.rearrange("k (r t) -> r k t", t=P), nrow[:]).then_inc(m_out, 16)
                            act.wait_ge(m_out, 64 * it + 16 * n + 16)
                            act.dma_start(qs[ROWS:ROWS + NM, n], rows_dram.rearrange("k (j t) -> k j t", j=HG)).then_inc(m_rows, 16)
                        for u in range(4 * n):
                            exp(it, n, u, False)
                        with act.If(slow > 0):
                            for u in range(4 * n, 4 * n + 4):
                                exp(it, n, u, True)
                        with act.If(slow < 1):
                            for u in range(4 * n, 4 * n + 4):
                                exp(it, n, u, False)

                groups(act, group)

            @block.vector
            def _(dve):
                slow = dve.value_load(flag[0:1, 0:1], min_val=0, max_val=1)
                nc.vector.memset(qs[ROWS:ROWS + NM], 0.0).then_inc(stacks_ready, 1)
                nc.vector.memset(ks[ROWS:ROWS + NM], 1.0).then_inc(stacks_ready, 1)
                dve.wait_ge(consts_in, 96)

                def maxima(it, n, slot):
                    bx = 4 * it + n
                    for i in range(TPB):
                        for j in range(HG):
                            dve.wait_ge(m_up, 16 * bx + 4 * i + j + 1)
                            width = (4 * n + i + 1) * P
                            ins = nc.vector.tensor_reduce(nmax[:, j * TPB + i:j * TPB + i + 1],
                                                          s_ps[:].rearrange("p a t -> p (a t)")[:, 0:width], AX.X, ALU.max, negate=True)
                            ins.then_inc(m_read, 1)
                    dve.wait_ge(mt_up, bx + 1)
                    at_least(dve, m_rows, 16 * bx)
                    turned = w_ps[0:HG * TPB, 0:P]
                    nc.vector.tensor_copy(nrow[:, 0], turned).then_inc(mt_parts, 1)
                    dve.wait_ge(mt_parts, 3 * bx + 1)
                    nc.vector.tensor_tensor(nsplit[:], turned, nrow[:, 0], ALU.subtract).then_inc(m_chain, 1)
                    dve.wait_ge(m_chain, bx + 1)
                    nc.vector.tensor_copy(nrow[:, 1], nsplit[:]).then_inc(mt_parts, 1)
                    dve.wait_ge(mt_parts, 3 * bx + 2)
                    nc.vector.tensor_tensor(nrow[:, 2], nsplit[:], nrow[:, 1], ALU.subtract).then_inc(mt_parts, 1)

                def o_evac(bx, par, unit_end):
                    dve.wait_ge(pv_done, unit_end)
                    nc.vector.tensor_copy(ot[:], o_ps[par][:]).then_inc(o_read, 1)

                def mask(unit, u, t0):
                    for h in range(2):
                        dve.wait_ge(probs_ready, 2 * unit + h + 1)
                        tile = pr[:, u % PRING, h, :, t0:t0 + P]
                        nc.vector.tensor_tensor(tile, tile, causal[:].unsqueeze(1).to_broadcast([P, 2, P]), ALU.min).then_inc(masked, 1)

                def task(name, bx, n, wn, xn_):
                    if name[0] == "A":
                        c = int(name[1])
                        dve.wait_ge(w_up, wn + 1)
                        nc.vector.tensor_tensor(am[:, n % 2, c], w_ps[:].rearrange("p (j t) -> p j t", j=HG),
                                                before[:].unsqueeze(1).to_broadcast([P, HG, P]), ALU.mult).then_inc(w_read, 1)
                    elif name == "T":
                        dve.wait_ge(w_up, wn + 1)
                        o4 = w_ps[:].rearrange("p (i j c) -> p i j c", i=TPB, j=HG)
                        at_least(dve, w_read, wn)
                        nc.vector.reciprocal(inv[:], o4[:, :, :, D]).then_inc(chain_s, 1)
                        dve.wait_ge(chain_s, 2 * bx + 1)
                        nc.vector.tensor_tensor(y[:], o4[:, :, :, 0:D], inv[:].unsqueeze(3).to_broadcast([P, TPB, HG, D]), ALU.mult).then_inc(w_read, 1)
                    elif name == "G":
                        dve.wait_ge(x_up, xn_ + 1)
                        at_least(dve, run_ready, 4 * bx)
                        nc.vector.tensor_tensor(gm[:], x_ps[0:CG].rearrange("p (i c) -> p i c", i=TPB),
                                                own[:].unsqueeze(1).to_broadcast([CG, TPB, P]), ALU.mult).then_inc(x_read, 1)
                        if n == 0:
                            nc.vector.memset(run[:, 0], 0.0).then_inc(chain_s, 1)
                        else:
                            nc.vector.tensor_copy(run[:, 0], run[:, TPB]).then_inc(chain_s, 1)
                        dve.wait_ge(x_read, xn_ + 1)
                        dve.wait_ge(chain_s, 2 * bx + 2)
                        for c in range(TPB):
                            if c:
                                dve.wait_ge(run_ready, 4 * bx + c)
                            nc.vector.tensor_tensor(run[:, c + 1], run[:, c], gm[:, c], ALU.add).then_inc(run_ready, 1)
                    elif name == "Y":
                        dve.wait_ge(x_up, xn_ + 1)
                        nc.vector.tensor_copy(y2t[:], x_ps[:]).then_inc(x_read, 1)
                    else:
                        dve.wait_ge(w_up, wn + 1)
                        grp = bx // 4
                        o4 = w_ps[:].rearrange("p (i j c) -> p i j c", i=TPB, j=HG)
                        out = z[:, ds(grp * (T // P) + 4 * n, TPB), :].rearrange("p i (j d) -> p i j d", d=D)
                        nc.vector.tensor_tensor(out, o4[:, :, :, 0:D], y[:], ALU.add).then_inc(w_read, 1)

                def group(it, slot, rnd):
                    for n in range(NQ):
                        bx = 4 * it + n
                        with dve.If(slow > 0):
                            maxima(it, n, slot)
                        for u in range(4 * n + 4):
                            if u == LAG - 1 and not (isinstance(bx, int) and bx == 0):
                                o_evac(bx - 1, (n - 1) % 2, UNITS * it + UB[n])
                            for step in tasks(it, UB[n] + u):
                                task(*step)
                            if u >= 4 * n:
                                mask(UNITS * it + UB[n] + u, u, (u - 4 * n) * P)

                groups(dve, group)
                o_evac(4 * NG - 1, 1, UNITS * NG)
                wn, xn_ = W_END, X_END
                for name in LAST:
                    task(name, 4 * NG - 1, NQ - 1, wn, xn_)
                    wn, xn_ = wn + (name in "TZ"), xn_ + (name in "GY")

            @block.tensor
            def _(pe):
                slow = pe.value_load(flag[0:1, 0:1], min_val=0, max_val=1)
                pe.wait_ge(consts_in, 96)
                pe.wait_ge(pads_ready, 4)

                def maxima(it, n, slot):
                    bx = 4 * it + n
                    at_least(pe, probs_ready, 2 * (UNITS * it + UB[n]))
                    for i in range(TPB):
                        for j in range(HG):
                            at_least(pe, m_read, 16 * bx + 4 * i + j)
                            for blk in range(n + 1):
                                width = min(BLK, (4 * n + i + 1) * P - blk * BLK)
                                nc.tensor.matmul(s_ps[:, blk, 0:width], qs[0:ROWS, n, j, i * P:i * P + P],
                                                 ks[0:ROWS, slot, j, blk * BLK:blk * BLK + width], start=True, stop=(blk < n))
                            nc.tensor.matmul(s_ps[:, n, i * P:i * P + P], idb[:], later_t[:], start=False, stop=True).then_inc(m_up, 1)
                    pe.wait_ge(m_read, 16 * bx + 16)
                    at_least(pe, w_read, used(W_STEPS, it, sum(st[0] < UB[n] for st in SCHEDULE if st[1] not in ("G", "Y"))))
                    nc.tensor.transpose(w_ps[0:HG * TPB, 0:P], nmax[:], idf[:]).then_inc(mt_up, 1)
                    pe.wait_ge(m_rows, 16 * bx + 16)

                def scores(it, n, slot, u, h):
                    unit = UNITS * it + UB[n] + u
                    t0 = max(0, (u - 4 * n) * P)
                    at_least(pe, probs_ready, 2 * unit + h - 1)
                    for j in (2 * h, 2 * h + 1):
                        last = nc.tensor.matmul(s_ps[:, j, t0:], ks[:, slot, j, u * P:u * P + P], qs[:, n, j, t0:], start=True, stop=True)
                    last.then_inc(scores_up, 1)

                def values(it, n, slot, u):
                    unit = UNITS * it + UB[n] + u
                    t0 = max(0, (u - 4 * n) * P)
                    pe.wait_ge(probs_ready, 2 * unit + 2)
                    if u >= 4 * n:
                        pe.wait_ge(masked, 8 * (4 * it + n) + 2 * (u - 4 * n) + 2)
                    if u == 0:
                        pe.wait_ge(va_ready, it + 1)
                        at_least(pe, o_read, 4 * it + n - 1)
                    for j in range(HG):
                        last = nc.tensor.matmul(o_ps[n % 2][PAD * j:PAD * (j + 1), t0:], va[:, slot, u, j], pr[:, u % PRING, j // 2, j % 2, t0:],
                                                start=(u == 0), stop=(u == 4 * n + 3), tile_position=(0, PAD * j), skip_group_check=True)
                    last.then_inc(pv_done, 1)

                def task(name, bx, n, wn, xn_):
                    if name[0] == "A":
                        c = int(name[1])
                        at_least(pe, w_read, wn)
                        if c == 0:
                            pe.wait_ge(as_in[n % 2], 96 * bx - 96 * (n % 2) + 192)
                        for j in range(HG):
                            last = nc.tensor.matmul(w_ps[:, j * P:j * P + P], kas[:, n % 2, j, c * P:c * P + P],
                                                    qas[:, n % 2, j, c * P:c * P + P], start=True, stop=True)
                        last.then_inc(w_up, 1)
                    elif name in "TZ":
                        src = ot if name == "T" else y2t
                        if name == "T":
                            pe.wait_ge(o_read, bx + 1)
                        else:
                            pe.wait_ge(x_read, xn_)
                        at_least(pe, w_read, wn)
                        for i in range(TPB):
                            last = nc.tensor.transpose(w_ps[:, i * P:i * P + P], src[:, i * P:i * P + P], idf[:])
                        last.then_inc(w_up, 1)
                    elif name == "G":
                        pe.wait_ge(e_ready, bx + 1)
                        pe.wait_ge(lin_in[n % 2], 24 * bx - 24 * (n % 2) + 48)
                        at_least(pe, x_read, xn_)
                        for c in range(TPB):
                            last = nc.tensor.matmul(x_ps[0:CG, c * P:c * P + P], kan[:, n % 2, c], e[:, c].rearrange("p j d -> p (j d)"), start=True, stop=True)
                        last.then_inc(x_up, 1)
                    else:
                        pe.wait_ge(run_ready, 4 * bx + 4)
                        pe.wait_ge(x_read, xn_)
                        pe.wait_ge(w_read, wn)
                        for c in range(TPB):
                            nc.tensor.matmul(x_ps[:, c * P:c * P + P], run[:, c], qap[:, n % 2, c * P:c * P + P], start=(c == 0), stop=False, skip_group_check=True)
                            for j in range(HG):
                                last = nc.tensor.matmul(x_ps[PAD * j:PAD * (j + 1), c * P:c * P + P], e[:, c, j], am[:, n % 2, c, j],
                                                        start=False, stop=(c == TPB - 1), tile_position=(0, PAD * j), skip_group_check=True)
                        last.then_inc(x_up, 1)

                def group(it, slot, rnd):
                    pe.wait_ge(ks_in[slot], 96 * rnd + 96)
                    for n in range(NQ):
                        bx = 4 * it + n
                        pe.wait_ge(qs_in[n], 96 * it + 96)
                        with pe.If(slow > 0):
                            maxima(it, n, slot)
                        for u in range(4 * n + 4):
                            scores(it, n, slot, u, 0)
                            if u >= LAG:
                                values(it, n, slot, u - LAG)
                            elif n:
                                values(it, n - 1, slot, 4 * n + u - LAG)
                            elif not (isinstance(it, int) and it == 0):
                                values(it - 1, NQ - 1, 1 - slot, 4 * NQ + u - LAG)
                            scores(it, n, slot, u, 1)
                            for step in tasks(it, UB[n] + u):
                                task(*step)

                pe.wait_ge(stacks_ready, 2)
                groups(pe, group)
                for u in range(4 * NQ - LAG, 4 * NQ):
                    values(NG - 1, NQ - 1, 1, u)
                wn, xn_ = W_END, X_END
                for name in LAST:
                    task(name, 4 * NG - 1, NQ - 1, wn, xn_)
                    wn, xn_ = wn + (name in "TZ"), xn_ + (name in "GY")


TURN_Z, PROJECT = 1, 3


def finish(nc, cst, z, x, w_proj, w_gate, w_up, w_down, out):
    with ExitStack() as ctx:
        sb = lambda name, shape, dt: ctx.enter_context(nc.sbuf_tensor(name, shape, dt))
        ps = lambda name, shape: ctx.enter_context(nc.psum_tensor(name, shape, F32))
        sem = lambda name: ctx.enter_context(nc.semaphore(name))
        idf = sb("ident_c", [P, P], F32)
        wp = sb("w_proj_sb", [P, KT, C], F32)
        wi = sb("w_int", [P, 3, KT * HID], I32)
        wg = sb("w_gate_sb", [P, KT, HID], F16)
        wu = sb("w_up_sb", [P, KT, HID], F16)
        wd = sb("w_down_sb", [P, NH, C], F32)
        x4 = sb("x_again", [P, TPB, C], F32)
        x1 = sb("x1", [P, NTOK // P, C], F32)
        zs = sb("z_block", [P, TPB, C], F32)
        zt = sb("z_t", [P, KT, BLK], F32)
        a = sb("attended", [P, TPB, C], F32)
        xs = sb("x1n_block", [P, TPB, C], F32)
        xh = sb("x1n_t_hi", [P, KT, BLK], F16)
        xl = sb("x1n_t_lo", [P, KT, BLK], F16)
        sg = sb("silu_gate", [P, 2, BLK], F32)
        h = sb("hidden", [P, NH, BLK], F32)
        f = sb("fed", [P, TPB, C], F32)
        yo = sb("out_block", [P, TPB, C], F32)
        st = [sb(f"st_c{i}", [P, TPB, 6], F32) for i in range(3)]
        mv = [sb(f"mv_c{i}", [P, TPB, 2], F32) for i in range(3)]
        nt = [[sb(f"nt_c{i}{k}", [P, TPB], F32) for k in range(3)] for i in range(3)]
        t_ps = ps("t_ps", [P, KT, BLK])
        a_ps = ps("a_ps", [P, TPB, C])
        g_ps = ps("g_ps", [P, 2, BLK])
        u_ps = ps("up_ps", [P, 2, BLK])

        idle = sem("idle_c")
        fp_in, int_in, w_ready = sem("fp_in"), [sem(f"int_in{i}") for i in range(3)], sem("w_ready")
        x_in, z_ready, z_up, zt_ready, a_up, a_ready = sem("x_again_in"), sem("zs_ready"), sem("z_up"), sem("zt_ready"), sem("a_up"), sem("a_ready")
        a_normed, x1_ready, xs_ready, xt_up, hi_ready, lo_ready = sem("a_normed"), sem("x1_ready"), sem("xs_ready"), sem("x1t_up"), sem("x1_hi"), sem("x1_lo")
        gu_up, silu_ready, h_ready, f_up, f_ready, f_normed = sem("gu_up"), sem("silu_ready"), sem("h_ready"), sem("f_up"), sem("f_ready"), sem("f_normed")
        out_ready, stored = sem("out_ready"), sem("out_stored")
        chains = [sem(f"chain_c{i}") for i in range(3)]

        def at_least(engine, s, value):
            if not isinstance(value, int) or value > 0:
                engine.wait_ge(s, value)

        def blocks(engine, body):
            body(0, 2)
            with engine.Fori(1, NBLK - 2) as n:
                body(n, 2)
            body(NBLK - 2, 1)
            body(NBLK - 1, 0)

        def rows(dram, n):
            return dram[ds(n * BLK, BLK), :].rearrange("(i p) c -> p i c", p=P)

        with nc.Block() as block:

            @block.sync
            def _(sp):
                def load_x(n):
                    hold(sp, x1_ready, n, idle)
                    sp.dma_start(x4[:], rows(x, n)).then_inc(x_in, 16)

                def store(n):
                    hold(sp, out_ready, n + 1, idle)
                    sp.dma_start(rows(out, n), yo[:]).then_inc(stored, 16)

                def body(n, ahead):
                    if ahead == 2:
                        load_x(n + 2)
                    if not (isinstance(n, int) and n == 0):
                        store(n - 1)

                sp.dma_start(idf[:], cst["ident"]).then_inc(fp_in, 16)
                sp.dma_start(wp[:], w_proj.rearrange("(k p) m -> p k m", p=P)).then_inc(fp_in, 16)
                load_x(0)
                for i, (w, k) in enumerate(((w_gate, KT), (w_up, KT), (w_down, NH))):
                    sp.dma_start(wi[:, i].rearrange("p (k m) -> p k m", k=k), w.rearrange("(k p) m -> p k m", p=P)).then_inc(int_in[i], 16)
                load_x(1)
                blocks(sp, body)
                store(NBLK - 1)
                sp.wait_ge(stored, 16 * NBLK)

            @block.gpsimd
            def _(pool):
                def stage_z(n):
                    hold(pool, z_up, n, idle)
                    for g in range(C // CG):
                        ins = nc.gpsimd.tensor_copy(zs[:, :, g * CG:(g + 1) * CG], z[:, ds((n // NQ * (C // CG) + g) * (T // P) + n % NQ * TPB, TPB), :])
                        ins.then_inc(z_ready, 1)

                def total(n):
                    pool.wait_ge(f_normed, 4 * n + 4)
                    at_least(pool, stored, 16 * n)
                    nc.gpsimd.tensor_tensor(yo[:], f[:], x1[:, ds(n * TPB, TPB), :], ALU.add).then_inc(out_ready, 1)

                def body(n, ahead):
                    if ahead == 2:
                        stage_z(n + 2)
                    if not (isinstance(n, int) and n == 0):
                        total(n - 1)

                stage_z(0)
                stage_z(1)
                blocks(pool, body)
                total(NBLK - 1)

            @block.scalar
            def _(act):
                def weights(dst, i):
                    act.wait_ge(int_in[i], 16)
                    nc.scalar.copy(dst[:].rearrange("p k m -> p (k m)"), wi[:, i]).then_inc(w_ready, 1)

                def z_turned(n):
                    act.wait_ge(z_up, n + 1)
                    at_least(act, a_up, n)
                    nc.scalar.copy(zt[:], t_ps[:]).then_inc(zt_ready, 1)

                def attended(n):
                    act.wait_ge(a_up, n + 1)
                    at_least(act, x1_ready, n)
                    nc.scalar.copy(a[:], a_ps[:]).then_inc(a_ready, 1)

                def x_turned(n):
                    act.wait_ge(xt_up, n + 1)
                    at_least(act, gu_up, NH * n)
                    nc.scalar.copy(xh[:], t_ps[:]).then_inc(hi_ready, 1)

                def body(n, ahead):
                    for m in range(NH):
                        act.wait_ge(gu_up, NH * n + m + 1)
                        at_least(act, h_ready, NH * n + m - 1)
                        nc.scalar.activation(sg[:, m % 2], g_ps[:, m % 2], ACT.Silu, scale=WSCALE).then_inc(silu_ready, 1)
                        if ahead == 2 and m == TURN_Z:
                            z_turned(n + 2)
                        if ahead == 2 and m == PROJECT:
                            attended(n + 2)
                    if ahead:
                        x_turned(n + 1)
                    act.wait_ge(f_up, n + 1)
                    at_least(act, out_ready, n)
                    nc.scalar.mul(f[:], a_ps[:], WSCALE).then_inc(f_ready, 1)

                z_turned(0)
                attended(0)
                z_turned(1)
                weights(wg, 0)
                weights(wu, 1)
                attended(1)
                x_turned(0)
                weights(wd, 2)
                blocks(act, body)

            @block.vector
            def _(dve):
                def normed(dst, src, which, i):
                    return nc.vector.tensor_scalar(dst, src, mv[which][:, i, 0:1], mv[which][:, i, 1:2], ALU.subtract, ALU.mult)

                def tile_of_x1(n, i):
                    return x1[:, ds(n * TPB + i, 1), :].rearrange("p a c -> p (a c)")

                def residual(n):
                    chain = Steps(dve, chains[0], LN_STEPS * n)
                    dve.wait_ge(a_ready, n + 1)
                    ln_moments(nc, chain, [a[:, i, :] for i in range(TPB)], st[0], mv[0], idle)
                    ln_rsqrt(nc, chain, mv[0], nt[0])
                    for i in range(TPB):
                        normed(a[:, i, :], a[:, i, :], 0, i).then_inc(a_normed, 1)
                    dve.wait_ge(a_normed, 4 * n + 4)
                    dve.wait_ge(x_in, 16 * n + 16)
                    nc.vector.tensor_tensor(x1[:, ds(n * TPB, TPB), :], x4[:], a[:], ALU.add).then_inc(x1_ready, 1)

                def second_norm(n):
                    chain = Steps(dve, chains[1], LN_STEPS * n)

                    def moments():
                        hold(dve, x1_ready, n + 1, idle)
                        ln_moments(nc, chain, [tile_of_x1(n, i) for i in range(TPB)], st[1], mv[1], idle)

                    def scaled():
                        at_least(dve, xt_up, n)
                        for i in range(TPB):
                            normed(xs[:, i, :], tile_of_x1(n, i), 1, i).then_inc(xs_ready, 1)

                    return [moments, lambda: ln_rsqrt(nc, chain, mv[1], nt[1]), scaled]

                def low_part(n):
                    dve.wait_ge(hi_ready, n + 1)
                    at_least(dve, gu_up, NH * n)
                    nc.vector.tensor_tensor(xl[:], t_ps[:], xh[:], ALU.subtract).then_inc(lo_ready, 1)

                def last_norm(n):
                    dve.wait_ge(f_ready, n + 1)
                    chain = Steps(dve, chains[2], LN_STEPS * n)
                    ln_moments(nc, chain, [f[:, i, :] for i in range(TPB)], st[2], mv[2], idle)
                    ln_rsqrt(nc, chain, mv[2], nt[2])
                    for i in range(TPB):
                        normed(f[:, i, :], f[:, i, :], 2, i).then_inc(f_normed, 1)

                def body(n, ahead):
                    pieces = second_norm(n + 1) if ahead else []
                    for m in range(NH):
                        dve.wait_ge(silu_ready, NH * n + m + 1)
                        at_least(dve, f_up, n)
                        nc.vector.scalar_tensor_tensor(h[:, m], u_ps[:, m % 2], WSCALE, sg[:, m % 2], ALU.mult, ALU.mult).then_inc(h_ready, 1)
                        if m < len(pieces):
                            pieces[m]()
                    if ahead:
                        low_part(n + 1)
                    if not (isinstance(n, int) and n == 0):
                        last_norm(n - 1)
                    if ahead == 2:
                        residual(n + 2)

                residual(0)
                for piece in second_norm(0):
                    piece()
                low_part(0)
                residual(1)
                blocks(dve, body)
                last_norm(NBLK - 1)

            @block.tensor
            def _(pe):
                def turn_z(n):
                    pe.wait_ge(z_ready, 4 * n + 4)
                    if isinstance(n, int) and n < 2:
                        at_least(pe, zt_ready, n)
                    else:
                        pe.wait_ge(lo_ready, n - 1)
                    for i in range(TPB):
                        for k in range(KT):
                            last = nc.tensor.transpose(t_ps[:, k, i * P:i * P + P], zs[:, i, k * P:k * P + P], idf[:])
                    last.then_inc(z_up, 1)

                def project_z(n):
                    pe.wait_ge(zt_ready, n + 1)
                    at_least(pe, a_ready, n)
                    if not (isinstance(n, int) and n < 3):
                        pe.wait_ge(f_ready, n - 2)
                    for i in range(TPB):
                        for k in range(KT):
                            last = nc.tensor.matmul(a_ps[:, i], zt[:, k, i * P:i * P + P], wp[:, k], start=(k == 0), stop=(k == KT - 1))
                    last.then_inc(a_up, 1)

                def turn_x(n):
                    pe.wait_ge(xs_ready, 4 * n + 4)
                    for i in range(TPB):
                        for k in range(KT):
                            last = nc.tensor.transpose(t_ps[:, k, i * P:i * P + P], xs[:, i, k * P:k * P + P], idf[:])
                    last.then_inc(xt_up, 1)

                def body(n, ahead):
                    pe.wait_ge(lo_ready, n + 1)
                    for m in range(NH):
                        at_least(pe, h_ready, NH * n + m - 1)
                        for w, bank in ((wg, g_ps), (wu, u_ps)):
                            for k in range(KT):
                                for part in (xh, xl):
                                    last = nc.tensor.matmul(bank[:, m % 2], w[:, k, m * P:m * P + P], part[:, k],
                                                            start=(k == 0 and part is xh), stop=(k == KT - 1 and part is xl))
                        last.then_inc(gu_up, 1)
                        if ahead == 2 and m == TURN_Z:
                            turn_z(n + 2)
                        if ahead == 2 and m == PROJECT:
                            project_z(n + 2)
                    if ahead:
                        turn_x(n + 1)
                    pe.wait_ge(h_ready, NH * n + NH)
                    pe.wait_ge(a_ready, n + 1 + ahead)
                    for i in range(TPB):
                        for k in range(NH):
                            last = nc.tensor.matmul(a_ps[:, i], h[:, k, i * P:i * P + P], wd[:, k], start=(k == 0), stop=(k == NH - 1))
                    last.then_inc(f_up, 1)

                pe.wait_ge(fp_in, 32)
                for n in range(2):
                    turn_z(n)
                    project_z(n)
                turn_x(0)
                pe.wait_ge(w_ready, 3)
                blocks(pe, body)


def layer(nc, t):
    parts = nc.dram_tensor("parts_dram", (4, 3, B * C, T), BF16, kind="Internal").ap()
    qa32 = nc.dram_tensor("qa32_dram", (B * C, T), F32, kind="Internal").ap()
    ka_nat = nc.dram_tensor("ka_nat_dram", (NG * T, CG), F32, kind="Internal").ap()
    xn_dram = nc.dram_tensor("xn_dram", (NG * T + 1, CG), F32, kind="Internal").ap()
    rows_dram = nc.dram_tensor("minus_max_dram", (NM, HG * BLK), BF16, kind="Internal").ap()
    with nc.sbuf_tensor("flag", [1, 1], I32) as flag, nc.sbuf_tensor("z", [P, NG * T // P, CG], F32) as z:
        project(nc, t["x"], t["w_attn"], t["w_k2"], t["ident"], t["heads"], flag, parts, qa32, ka_nat, xn_dram)
        attend(nc, t, flag, z, parts, qa32, ka_nat, xn_dram, rows_dram)
        finish(nc, t, z, t["x"], t["w_proj"], t["w_gate"], t["w_up"], t["w_down"], t["out"])


def kernel(**inputs):
    import ml_dtypes
    import numpy as np
    import concourse.bacc as bacc
    from concourse.bass_utils import run_bass_kernel_spmd

    bf16 = ml_dtypes.bfloat16
    i = np.arange(P)
    own = np.zeros((CG, P), np.float32)
    for j in range(HG):
        own[j * D:(j + 1) * D, j * PAD:j * PAD + D] = 1
    arrays = {
        "x": np.ascontiguousarray(inputs["L0_attn_x"]).reshape(NTOK, C),
        "w_attn": np.ascontiguousarray(inputs["L0_attn_W_attn"]),
        "w_k2": np.ascontiguousarray(inputs["L0_attn_W_k2"]),
        "w_proj": np.ascontiguousarray(inputs["L0_attn_W_proj"]),
        "w_gate": np.ascontiguousarray(np.asarray(inputs["L0_ffn_w_gate"]).T),
        "w_up": np.ascontiguousarray(np.asarray(inputs["L0_ffn_w_up"]).T),
        "w_down": np.ascontiguousarray(np.asarray(inputs["L0_ffn_w_down"]).T),
        "ident": np.eye(P, dtype=np.float32),
        "ident_bf": np.eye(P).astype(bf16),
        "heads": np.repeat(np.eye(P // D, dtype=np.float32), D, axis=0),
        "causal": np.where(i[:, None] > i[None, :], 0.0, np.finfo(np.float32).max).astype(np.float32),
        "later_t": np.where(i[:, None] < i[None, :], NEG, 0.0).astype(bf16),
        "before": (i[:, None] < i[None, :]).astype(np.float32),
        "own": own,
    }
    nc = bacc.Bacc("TRN2", target_bir_lowering=False, num_devices=1)
    t = {name: nc.dram_tensor(f"in_{name}", a.shape, mybir.dt.from_np(a.dtype), kind="ExternalInput").ap()
         for name, a in arrays.items()}
    t["out"] = nc.dram_tensor("out", (NTOK, C), F32, kind="ExternalOutput").ap()
    layer(nc, t)
    r = run_bass_kernel_spmd(nc, [{f"in_{name}": a for name, a in arrays.items()}], core_ids=[0])
    return r.results[0]["out"].reshape(B, T, C)
```

```python
from contextlib import ExitStack

import concourse.bass as bass
from concourse import mybir

P = 128
BLK = 512
TPB = BLK // P
B, T, C = 2, 2048, 256
NTOK = B * T
NBLK = NTOK // BLK
NQ = T // BLK
H, D = 16, 16
HG = 4
CG = HG * D
HID = 768
NH = HID // P
KT = C // P
PAD = 32
TERMS = ((0, 0), (0, 1), (1, 0), (0, 2), (2, 0), (1, 1))
ROWS = D * len(TERMS)
NM = 3
SCALE = 1.0 / D ** 0.5
MA_SCALE = 0.02 * SCALE
LEAK = 0.02 * SCALE
KA, Q, K, QA = range(4)
WSCALE = 1.0 / 127.0
EPS = 1e-5
SAFE = 75.0
NEG = -1e30

ALU = mybir.AluOpType
ACT = mybir.ActivationFunctionType
F32, BF16, F16, I32 = mybir.dt.float32, mybir.dt.bfloat16, mybir.dt.float16, mybir.dt.int32
AX = mybir.AxisListType
ds = bass.ds


def hold(engine, sem, value, idle):
    if not isinstance(value, int) or value > 0:
        engine.wait_ge(sem, value)
        engine.sem_inc(idle, 1)


LN_STEPS = 14


def ln_moments(nc, dve, sem, base, rows, st, mv, idle):
    for i, row in enumerate(rows):
        if i == len(rows) // 2:
            yield
        ins = nc.vector.bn_stats(st[:, i, :], row)
    ins.then_inc(sem, 1)
    hold(dve, sem, base + 1, idle)
    for i in range(len(rows)):
        ins = nc.vector.bn_aggr(mv[:, i, :], st[:, i, :])
    ins.then_inc(sem, 1)


def ln_rsqrt(nc, dve, sem, base, mv, nt):
    v, y, t = nt
    steps = [lambda: nc.vector.tensor_scalar(v[:], mv[:, :, 1], EPS, None, ALU.add),
             lambda: nc.vector.tensor_scalar(t[:].bitcast(I32), v[:].bitcast(I32), 1, None, ALU.logical_shift_right),
             lambda: nc.vector.tensor_scalar(y[:].bitcast(I32), t[:].bitcast(I32), -1.0, float(0x5F3759DF), ALU.mult, ALU.add)]
    for k in range(3):
        steps += [lambda: nc.vector.tensor_tensor(t[:], y[:], y[:], ALU.mult),
                  lambda: nc.vector.scalar_tensor_tensor(t[:], t[:], -0.5, v[:], ALU.mult, ALU.mult),
                  lambda out=y[:] if k < 2 else mv[:, :, 1]: nc.vector.scalar_tensor_tensor(out, t[:], 1.5, y[:], ALU.add, ALU.mult)]
    assert 2 + len(steps) == LN_STEPS
    for k, step in enumerate(steps):
        dve.wait_ge(sem, base + 2 + k)
        step().then_inc(sem, 1)
        yield


def run_all(steps):
    for _ in steps:
        pass


def by_turns(*all_steps):
    left = list(all_steps)
    while left:
        for steps in list(left):
            if next(steps, left) is left:
                left.remove(steps)
            else:
                yield


def stack(queue, dst, parts, kind, side, it, cols, s):
    run_all(stack_terms(queue, dst, parts, kind, side, it, cols, s))


def stack_terms(queue, dst, parts, kind, side, it, cols, s):
    for r, term in enumerate(TERMS):
        queue.dma_start(dst[r * D:(r + 1) * D],
                        parts[kind, term[side], ds(it * CG, CG), cols].rearrange("(j d) t -> d j t", d=D)).then_inc(s, 16)
        yield


def copy_values(nc, sh, slot):
    return nc.gpsimd.tensor_copy(sh.va[:, slot, :, :, 0:D], sh.vraw[:].rearrange("p i (j d) -> p i j d", d=D))


def project(nc, t, sh, parts, qa32, ka_nat, xn_dram):
    x, w_qk, w_k2, idf, flag = t["x"], t["w_attn"], t["w_k2"], sh.idf, sh.flag
    with ExitStack() as ctx:
        sb = lambda name, shape, dt: ctx.enter_context(nc.sbuf_tensor(name, shape, dt))
        ps = lambda name, shape: ctx.enter_context(nc.psum_tensor(name, shape, F32))
        sem = lambda name: ctx.enter_context(nc.semaphore(name))
        w = sb("w_all", [P, KT, 3 * C], F32)
        ind = sb("head_of_channel", [P, P // D], F32)
        x4 = sb("x_block", [P, 2, TPB, C], F32)
        xs = sb("xn_block", [P, TPB, C], F32)
        xt = sb("xn_t", [P, 2, KT, BLK], F32)
        hi_lo = sb("parts_sb", [P, 8, 3, BLK], BF16)
        rest = sb("rest", [P, 8, BLK], F32)
        small = sb("q_leak", [P, 2, BLK], F32)
        qaf = sb("qa_f32", [P, 2, BLK], F32)
        kaf = sb("ka_f32", [P, 2, BLK], F32)
        kn = sb("ka_nat_sb", [P, TPB, C], F32)
        zrow = sb("zero_row", [1, C], F32)
        st = sb("st_a", [P, TPB, 6], F32)
        mv = sb("mv_a", [P, TPB, 2], F32)
        nt = [sb(f"nt_a{i}", [P, TPB], F32) for i in range(3)]
        peak = sb("peak", [P, 8, BLK], BF16)
        top = sb("peak_top", [P, 8], F32)
        prod = sb("peak_prod", [P, 2], F32)
        bound = sb("bound", [1, 1], F32)
        u = ps("u_ps", [P, 6, BLK])
        t_ps = ps("turned_ps", [P, KT * BLK])
        xt_ps, kn_ps = t_ps.rearrange("p (k t) -> p k t", k=KT), t_ps.rearrange("p (i c) -> p i c", i=TPB)

        idle = sem("idle_a")
        w_in, x_in, xn_done, xt_up, xt_down = sem("w_in"), [sem("x_in0"), sem("x_in1")], sem("xn_done"), sem("xt_up"), sem("xt_down")
        u_ready = sem("u_ready")
        hi_ready, leak_ready, kaf_ready, qaf_ready = sem("hi_ready"), sem("leak_ready"), sem("kaf_ready"), sem("qaf_ready")
        rest_ready, mid_dve, mid_act, lo_ready = sem("rest_ready"), sem("mid_dve"), sem("mid_act"), sem("lo_ready")
        kn_up, kn_down = sem("kn_up"), sem("kn_down")
        consts_in, first_in, v_in, pads_ready = sem("consts_in"), sem("first_in"), sem("v_in_a"), sem("pads_ready")
        stored = [sem(f"stored{s}") for s in range(8)]
        qa_stored, kn_stored, xn_stored, z_stored = [sem("qa_stored0"), sem("qa_stored1")], sem("kn_stored"), sem("xn_stored"), sem("z_stored")
        chain_s, peak_done, top_ready, prod_ready, sum_ready, z_ready, bound_ready = sem("chain_a"), sem("peak_done"), sem("top_ready"), sem("prod_ready"), sem("sum_ready"), sem("z_ready"), sem("bound_ready")

        def tokens(dram, n):
            return dram[ds(n * BLK, BLK), :].rearrange("(i p) c -> p i c", p=P)

        def blocks(engine, body):
            with engine.Fori(0, NBLK // 2 - 1) as i:
                body(2 * i, 0, 2)
                body(2 * i + 1, 1, 2)
            body(NBLK - 2, 0, 1)
            body(NBLK - 1, 1, 0)

        def load_x(queue, n, buf):
            queue.dma_start(x4[:, buf], tokens(x, n)).then_inc(x_in[buf], 16)

        with nc.Block() as block:

            @block.sync
            def _(sp):
                def store_xn(n):
                    hold(sp, xn_done, 4 * n + 4, idle)
                    sp.dma_start(tokens(xn_dram, n), xs[:]).then_inc(xn_stored, 16)

                def body(n, buf, ahead):
                    if ahead:
                        store_xn(n + 1)
                    for s in range(8):
                        if ahead < 2:
                            next(early, None)
                        hold(sp, lo_ready, 8 * n + s + 1, idle)
                        sp.dma_start(parts[s // 2, :, ds(n // NQ * C + s % 2 * P, P), ds(n % NQ * BLK, BLK)].rearrange("a p t -> p a t"),
                                     hi_lo[:, s]).then_inc(stored[s], 16)
                        if s == 3:
                            for c in range(2):
                                hold(sp, qaf_ready, 2 * n + c + 3, idle)
                                sp.dma_start(qa32[ds(n // NQ * C + c * P, P), ds(n % NQ * BLK, BLK)], qaf[:, c]).then_inc(qa_stored[c], 16)
                        if s == 2:
                            hold(sp, kn_down, n + 2, idle)
                            sp.dma_start(tokens(ka_nat, n), kn[:]).then_inc(kn_stored, 16)

                def first_group():
                    for s in stored[2 * Q:2 * K + 2]:
                        hold(sp, s, 16 * (NBLK - 2) + 16, idle)
                    for m in range(EARLY):
                        cols = slice(m * BLK, m * BLK + BLK)
                        for dst, kind, side in ((sh.ks[:, 0, :, cols], K, 0), (sh.qs[:, m], Q, 1)):
                            for k, _ in enumerate(stack_terms(sp, dst, parts, kind, side, 0, cols, first_in)):
                                if k % 2:
                                    yield
                        if m == 0:
                            hold(sp, xn_stored, 16 * NBLK, idle)
                            sp.dma_start(sh.vraw[:], xn_dram[0:T, 0:CG].rearrange("(i p) c -> p i c", p=P)).then_inc(v_in, 16)

                early = first_group()
                load_x(sp, 0, 0)
                sp.dma_start(idf[:], t["ident"]).then_inc(w_in, 16)
                sp.dma_start(w[:, :, 0:C], w_k2.rearrange("(k p) m -> p k m", p=P)).then_inc(w_in, 16)
                sp.dma_start(w[:, :, C:], w_qk.rearrange("(k p) m -> p k m", p=P)).then_inc(w_in, 16)
                load_x(sp, 1, 1)
                sp.dma_start(ind[:], t["heads"]).then_inc(w_in, 16)
                for dst, name in ((sh.idb, "ident_bf"), (sh.causal, "causal"), (sh.later_t, "later_t"), (sh.before, "before"), (sh.own, "own")):
                    sp.dma_start(dst[:], t[name]).then_inc(consts_in, 16)
                store_xn(0)
                sp.wait_ge(z_ready, 1)
                sp.dma_start(xn_dram[NTOK:, :], zrow[:]).then_inc(z_stored, 16)
                for s in stored + qa_stored:
                    sp.sem_inc(s, 16)
                sp.sem_inc(kn_stored, 16)
                blocks(sp, body)
                for s in stored + qa_stored:
                    sp.wait_ge(s, 16 * NBLK + 16)
                sp.wait_ge(kn_stored, 16 * NBLK + 16)
                sp.wait_ge(first_in, 16 * 4 * len(TERMS))
                sp.wait_ge(consts_in, 80)
                sp.wait_ge(xn_stored, 16 * NBLK)
                sp.wait_ge(z_stored, 16)

            @block.vector
            def _(dve):
                nc.vector.memset(zrow[:], 0.0).then_inc(z_ready, 1)
                nc.vector.memset(peak[:], 0.0).then_inc(peak_done, 1)
                dve.sem_inc(rest_ready, 8)
                dve.sem_inc(qaf_ready, 2)

                def norm(n, buf):
                    dve.wait_ge(x_in[buf], 8 * (n - buf) + 16)
                    yield from ln_moments(nc, dve, chain_s, n * LN_STEPS, [x4[:, buf, i, :] for i in range(TPB)], st, mv, idle)
                    yield
                    yield from ln_rsqrt(nc, dve, chain_s, n * LN_STEPS, mv, nt)
                    dve.wait_ge(chain_s, (n + 1) * LN_STEPS)
                    if not (isinstance(n, int) and n == 0):
                        dve.wait_ge(xt_up, n)
                        dve.wait_ge(xn_stored, 16 * n)
                    for i in range(TPB):
                        nc.vector.tensor_scalar(xs[:, i, :], x4[:, buf, i, :],
                                                mv[:, i, 0:1], mv[:, i, 1:2], ALU.subtract, ALU.mult).then_inc(xn_done, 1)

                def body(n, buf, ahead):
                    between = norm(n + 2, buf) if ahead == 2 else iter(())
                    for s in range(8):
                        kind, c = s // 2, s % 2
                        dve.wait_ge(hi_ready, 8 * n + s + 1)
                        if kind == Q:
                            dve.wait_ge(leak_ready, 2 * n + c + 1)
                        f = kaf[:, c] if kind == KA else qaf[:, c] if kind == QA else u[:, s]
                        nc.vector.tensor_tensor(rest[:, s], f, hi_lo[:, s, 0], ALU.subtract).then_inc(rest_ready, 1)
                        if s:
                            next(between, None)
                        if kind == Q:
                            dve.wait_ge(qa_stored[c], 16 * n + 16)
                            dve.wait_ge(rest_ready, 8 * n + 2 * QA + c + 1)
                            nc.vector.scalar_tensor_tensor(qaf[:, c], u[:, s], SCALE, small[:, c], ALU.mult, ALU.min).then_inc(qaf_ready, 1)
                        if kind in (Q, K):
                            dve.wait_ge(peak_done, 4 * n + s - 1)
                            nc.vector.tensor_tensor(peak[:, s - 2], hi_lo[:, s, 0], peak[:, s - 2], ALU.max)
                            nc.vector.tensor_tensor(peak[:, s + 2], hi_lo[:, s, 0], peak[:, s + 2], ALU.min).then_inc(peak_done, 1)
                        if s:
                            next(between, None)
                        if s % 2 == 0:
                            dve.wait_ge(rest_ready, 8 * n + 8 + s + 1)
                            nc.vector.tensor_copy(hi_lo[:, s, 1], rest[:, s]).then_inc(mid_dve, 1)
                        if ahead == 0 and kind in (Q, K) and c == 1:
                            r = s - 3
                            dve.wait_ge(peak_done, 4 * n + s)
                            nc.vector.tensor_reduce(top[:, r:r + 2], peak[:, r:r + 2], AX.X, ALU.max)
                            nc.vector.tensor_reduce(top[:, 4 + r:6 + r], peak[:, 4 + r:6 + r], AX.X, ALU.min).then_inc(top_ready, 1)
                    if ahead == 0:
                        dve.wait_ge(top_ready, 2)
                        nc.vector.scalar_tensor_tensor(top[:, 0:4], top[:, 4:8], -1.0, top[:, 0:4], ALU.mult, ALU.max).then_inc(prod_ready, 1)
                        dve.wait_ge(prod_ready, 1)
                        nc.vector.tensor_tensor(prod[:], top[:, 0:2], top[:, 2:4], ALU.mult).then_inc(prod_ready, 1)
                    run_all(between)

                run_all(norm(0, 0))
                run_all(norm(1, 1))
                blocks(dve, body)
                dve.wait_ge(sum_ready, 1)
                nc.vector.tensor_reduce(bound[:], t_ps[0:1, 0:KT * P // D], AX.X, ALU.max).then_inc(bound_ready, 1)
                dve.wait_ge(bound_ready, 1)
                nc.vector.tensor_scalar(flag[:], bound[:], SCALE * 1.01, SAFE, ALU.mult, ALU.is_gt).then_inc(bound_ready, 1)

            @block.scalar
            def _(act):
                act.sem_inc(kaf_ready, 2)
                act.sem_inc(kn_down, 1)

                def xt_evac(n, buf):
                    act.wait_ge(xt_up, n + 1)
                    if not (isinstance(n, int) and n == 0):
                        act.wait_ge(u_ready, 6 * (n - 1) + 1)
                    nc.scalar.copy(xt[:, buf], xt_ps[:]).then_inc(xt_down, 1)

                def hi(n, s, src):
                    act.wait_ge(stored[s], 16 * n + 16)
                    nc.scalar.copy(hi_lo[:, s, 0], src).then_inc(hi_ready, 1)

                def mid(n, s):
                    act.wait_ge(rest_ready, 8 * n + 8 + s + 1)
                    nc.scalar.copy(hi_lo[:, s, 1], rest[:, s]).then_inc(mid_act, 1)

                def body(n, buf, ahead):
                    if ahead == 2:
                        hold(act, xn_done, 4 * n + 4, idle)
                        load_x(act, n + 2, buf)
                    for c in range(2):
                        act.wait_ge(u_ready, 6 * n + c + 2)
                        act.wait_ge(rest_ready, 8 * n + c + 1)
                        nc.scalar.activation(kaf[:, c], u[:, c], ACT.Sigmoid, scale=MA_SCALE).then_inc(kaf_ready, 1)
                    act.wait_ge(kaf_ready, 2 * n + 4)
                    for c in range(2):
                        hi(n, 2 * KA + c, kaf[:, c])
                    for s in (2, 3):
                        act.wait_ge(u_ready, 6 * n + s + 2)
                        hi(n, s, u[:, s])
                        nc.scalar.mul(small[:, s - 2], u[:, s], LEAK).then_inc(leak_ready, 1)
                        if s == 2:
                            mid(n, 1)
                            act.wait_ge(kn_up, n + 1)
                            act.wait_ge(kn_stored, 16 * n + 16)
                            nc.scalar.copy(kn[:], kn_ps[:]).then_inc(kn_down, 1)
                    for s in (4, 5):
                        act.wait_ge(u_ready, 6 * n + s + 2)
                        hi(n, s, u[:, s])
                        if s == 4:
                            mid(n, 3)
                            if ahead:
                                xt_evac(n + 1, 1 - buf)
                    for c in range(2):
                        act.wait_ge(qaf_ready, 2 * n + c + 3)
                        hi(n, 2 * QA + c, qaf[:, c])
                    mid(n, 5)
                    mid(n, 7)

                xt_evac(0, 0)
                blocks(act, body)

            @block.gpsimd
            def _(pool):
                def body(n):
                    for s in range(8):
                        pool.wait_ge(mid_dve if s % 2 == 0 else mid_act, 4 * n + s // 2 + 1)
                        nc.gpsimd.tensor_tensor(hi_lo[:, s, 2], rest[:, s], hi_lo[:, s, 1], ALU.subtract).then_inc(lo_ready, 1)

                for k, (dst, value) in enumerate([(sh.qs[ROWS:ROWS + NM], 0.0), (sh.ks[ROWS:ROWS + NM], 1.0), (sh.va[:], 0.0),
                                                  (sh.va[:, 0, :, :, D:D + 1], 1.0), (sh.va[:, 1, :, :, D:D + 1], 1.0)]):
                    if k:
                        pool.wait_ge(pads_ready, k)
                    nc.gpsimd.memset(dst, value).then_inc(pads_ready, 1)
                pool.wait_ge(pads_ready, 5)
                with pool.Fori(0, NBLK) as n:
                    body(n)
                pool.wait_ge(v_in, 16)
                copy_values(nc, sh, 0)

            @block.tensor
            def _(pe):
                pe.sem_inc(u_ready, 1)

                def turn_x(n):
                    pe.wait_ge(xn_done, 4 * n + 4)
                    if not (isinstance(n, int) and n == 0):
                        pe.wait_ge(kn_down, n + 1)
                    for i in range(TPB):
                        for k in range(KT):
                            last = nc.tensor.transpose(xt_ps[:, k, i * P:i * P + P], xs[:, i, k * P:k * P + P], idf[:])
                    last.then_inc(xt_up, 1)

                def turn_ka(n):
                    pe.wait_ge(kaf_ready, 2 * n + 4)
                    for i in range(TPB):
                        for k in range(KT):
                            last = nc.tensor.transpose(kn_ps[:, i, k * P:k * P + P], kaf[:, k, i * P:i * P + P], idf[:])
                    last.then_inc(kn_up, 1)

                def body(n, buf, ahead):
                    pe.wait_ge(xt_down, n + 1)
                    for m in range(6):
                        if m // 2 == KA:
                            pe.wait_ge(kaf_ready, 2 * n + m + 1)
                        elif m // 2 == Q:
                            pe.wait_ge(qaf_ready, 2 * n + m - 1)
                        else:
                            pe.wait_ge(rest_ready, 8 * n + m + 1)
                        for k in range(KT):
                            ins = nc.tensor.matmul(u[:, m], w[:, k, m * P:m * P + P], xt[:, buf, k], start=(k == 0), stop=(k == KT - 1))
                        ins.then_inc(u_ready, 1)
                        if m == 2:
                            turn_ka(n)
                        if m == 4 and ahead:
                            turn_x(n + 1)

                pe.wait_ge(w_in, 64)
                turn_x(0)
                blocks(pe, body)
                pe.wait_ge(prod_ready, 2)
                pe.wait_ge(kn_down, NBLK + 1)
                for k in range(KT):
                    last = nc.tensor.matmul(t_ps[0:1, k * (P // D):(k + 1) * (P // D)], prod[:, k:k + 1], ind[:], start=True, stop=True)
                last.then_inc(sum_ready, 1)


NG_B = C // CG
NG = B * NG_B
UB = [4 * n * (n + 1) // 2 for n in range(NQ + 1)]
UNITS = UB[NQ]
PRING = 4
EARLY = 2
LAG = 2
SCHEDULE = [(0, "A0", 0), (1, "A1", 0), (2, "T", -1), (3, "A2", 0), (4, "G", -1), (5, "A3", 0), (6, "Y", -1), (7, "Z", -1),
            (8, "T", 0), (9, "A0", 1), (10, "G", 0), (11, "Y", 0), (12, "A1", 1), (13, "Z", 0),
            (14, "T", 1), (15, "A2", 1), (16, "G", 1), (17, "A3", 1), (18, "Y", 1), (19, "Z", 1),
            (20, "A0", 2), (21, "A1", 2), (22, "A2", 2), (23, "A3", 2),
            (26, "T", 2), (27, "A0", 3), (28, "G", 2), (29, "A1", 3), (30, "Y", 2), (31, "Z", 2), (33, "A2", 3), (35, "A3", 3)]
LAST = "TGYZ"
W_STEPS = [step[1:] for step in SCHEDULE if step[1] not in ("G", "Y")]
X_STEPS = [step[1:] for step in SCHEDULE if step[1] in ("G", "Y")]


def used(steps, it, upto):
    if isinstance(it, int) and it == 0:
        return sum(m >= 0 for _, m in steps[:upto])
    return len(steps) * it + upto - sum(m < 0 for _, m in steps)


def used_with(steps, it, name, m):
    return used(steps, it, steps.index((name, m)) + 1)


def attend(nc, sh, parts, qa32, ka_nat, xn_dram, rows_dram):
    flag, z, idf, idb, causal, later_t, before, own = sh.flag, sh.z, sh.idf, sh.idb, sh.causal, sh.later_t, sh.before, sh.own
    ks, qs, vraw, va = sh.ks, sh.qs, sh.vraw, sh.va
    with ExitStack() as ctx:
        sb = lambda name, shape, dt: ctx.enter_context(nc.sbuf_tensor(name, shape, dt))
        ps = lambda name, shape: ctx.enter_context(nc.psum_tensor(name, shape, F32))
        sem = lambda name: ctx.enter_context(nc.semaphore(name))
        kas = sb("ka_stack", [ROWS, 2, HG, BLK], BF16)
        qas = sb("qa_stack", [ROWS, 2, HG, BLK], BF16)
        qap = sb("qa_plain", [CG, 2, BLK], F32)
        kan = sb("ka_tokens", [P, 2, TPB, CG], F32)
        vnext = sb("v_next", [P, 2, TPB, CG], F32)
        pr = sb("probs", [P, PRING, 2, 2, BLK], F32)
        am = sb("local_products", [P, 2, TPB, HG, P], F32)
        e = sb("e_padded", [P, TPB, HG, PAD], F32)
        ot = sb("y_t", [P, BLK], F32)
        y2t = sb("y2_t", [P, BLK], F32)
        inv = sb("inv_sum", [P, TPB, HG], F32)
        y = sb("y_tokens", [P, TPB, HG, D], F32)
        run = sb("running", [CG, TPB + 1, P], F32)
        gm = sb("ka_e", [CG, TPB, P], F32)
        nmax = sb("minus_max", [P, HG * TPB], F32)
        nsplit = sb("minus_max_rest", [HG * TPB, P], F32)
        nrow = sb("minus_max_parts", [HG * TPB, NM, P], BF16)
        s_ps = ps("s_ps", [P, 4, BLK])
        o_ps = [ps(f"o_ps{i}", [P, BLK]) for i in range(2)]
        w_ps = ps("w_ps", [P, BLK])
        x_ps = ps("x_ps", [P, BLK])

        idle = sem("idle_b")
        pads_ready = sem("pads_ready_b")
        ks_first = [sem(f"ks_first{i}") for i in range(NQ)]
        ks_in = [sem(f"ks_in{i}") for i in range(2)]
        qs_in = [sem(f"qs_in{i}") for i in range(NQ)]
        as_in = [sem(f"as_in{i}") for i in range(2)]
        lin_in = [sem(f"lin_in{i}") for i in range(2)]
        v_in, va_ready = sem("v_in"), sem("va_ready")
        scores_up, probs_ready, pv_done, o_read = sem("scores_up"), sem("probs_ready"), sem("pv_done"), sem("o_read")
        w_up, w_read, x_up, x_read = sem("w_up"), sem("w_read"), sem("x_up"), sem("x_read")
        masked, e_ready, run_ready, chain_s = sem("masked"), sem("e_ready"), sem("run_ready"), sem("chain_b")
        m_up, m_read, mt_up, mt_parts, m_out, m_rows, m_chain, clamped = sem("m_up"), sem("m_read"), sem("mt_up"), sem("mt_parts"), sem("m_out"), sem("m_rows"), sem("m_chain"), sem("clamped")

        def at_least(engine, s, value):
            if not isinstance(value, int) or value > 0:
                engine.wait_ge(s, value)

        def groups(engine, group):
            group(0, 0, 0)
            with engine.Fori(0, (NG - 2) // 2) as i:
                group(2 * i + 1, 1, i)
                group(2 * i + 2, 0, i + 1)
            group(NG - 1, 1, (NG - 1) // 2)

        def tasks(it, at):
            first = isinstance(it, int) and it == 0
            for unit, name, m in SCHEDULE:
                if unit == at and not (first and m < 0):
                    before_w = used(W_STEPS, it, sum(st[0] < at for st in SCHEDULE if st[1] not in ("G", "Y")))
                    before_x = used(X_STEPS, it, sum(st[0] < at for st in SCHEDULE if st[1] in ("G", "Y")))
                    yield name, 4 * it + m, m % NQ, before_w, before_x

        W_END, X_END = used(W_STEPS, NG, 0), used(X_STEPS, NG, 0)

        with nc.Block() as block:

            @block.sync
            def _(sp):
                def of_group(dram, it, start, count):
                    return dram[ds(it // NG_B * T + start, count), ds(it % NG_B * CG, CG)]

                def group(it, slot, rnd):
                    first = isinstance(it, int) and it == 0
                    if not first:
                        hold(sp, pv_done, UNITS * it - UNITS + 1, idle)
                        stack(sp, ks[:, slot], parts, K, 0, it, slice(0, T), ks_in[slot])
                        hold(sp, va_ready, it - 1, idle)
                        sp.dma_start(vraw[:], of_group(xn_dram, it, 0, T).rearrange("(i p) c -> p i c", p=P)).then_inc(v_in, 16)
                    for n in range(NQ):
                        bx = 4 * it + n
                        cols = slice(n * BLK, n * BLK + BLK)
                        if not (first and n < EARLY):
                            hold(sp, pv_done, UNITS * it - UNITS + UB[n + 1], idle)
                            stack(sp, qs[:, n], parts, Q, 1, it, cols, qs_in[n])
                        if first and n >= EARLY:
                            stack(sp, ks[:, slot, :, cols], parts, K, 0, it, cols, ks_first[n])
                        if not (first and n < 2):
                            other = (it, n - 2) if n >= 2 else (it - 1, n + 2)
                            hold(sp, w_read, used_with(W_STEPS, other[0], "A3", other[1]), idle)
                        stack(sp, kas[:, n % 2], parts, KA, 0, it, cols, as_in[n % 2])
                        stack(sp, qas[:, n % 2], parts, QA, 1, it, cols, as_in[n % 2])
                        if not (first and n < 2):
                            y_at = {0: (it - 1, 2), 1: (it, -1), 2: (it, 0), 3: (it, 1)}[n]
                            hold(sp, x_read, used_with(X_STEPS, y_at[0], "Y", y_at[1]), idle)
                        sp.dma_start(qap[:, n % 2], qa32[ds(it * CG, CG), cols]).then_inc(lin_in[n % 2], 16)
                        sp.dma_start(kan[:, n % 2], of_group(ka_nat, it, n * BLK, BLK).rearrange("(i p) c -> p i c", p=P)).then_inc(lin_in[n % 2], 16)
                        sp.dma_start(vnext[:, n % 2], of_group(xn_dram, it, n * BLK + 1, BLK).rearrange("(i p) c -> p i c", p=P)).then_inc(lin_in[n % 2], 16)

                groups(sp, group)

            @block.gpsimd
            def _(pool):
                nc.gpsimd.memset(e[:], 0.0).then_inc(pads_ready, 1)

                def values(it, slot):
                    pool.wait_ge(v_in, 16 * it)
                    hold(pool, pv_done, UNITS * it - UNITS, idle)
                    copy_values(nc, sh, slot).then_inc(va_ready, 1)

                def next_minus_y(bx, n, w_use):
                    pool.wait_ge(w_read, w_use + 1)
                    pool.wait_ge(lin_in[n % 2], 24 * bx - 24 * (n % 2) + 48)
                    nc.gpsimd.tensor_tensor(e[:, :, :, 0:D], vnext[:, n % 2].rearrange("p i (j d) -> p i j d", d=D), y[:], ALU.subtract).then_inc(e_ready, 1)

                def group(it, slot, rnd):
                    for at in range(UNITS):
                        for name, bx, n, wn, xn_ in tasks(it, at):
                            if name == "T":
                                next_minus_y(bx, n, wn)
                            if name == "T" and n == 2 and not (isinstance(it, int) and it == NG - 1):
                                values(it + 1, 1 - slot)

                groups(pool, group)
                next_minus_y(4 * NG - 1, NQ - 1, W_END)

            @block.scalar
            def _(act):
                slow = act.value_load(flag[0:1, 0:1], min_val=0, max_val=1)

                def exp(it, n, u, clamp):
                    unit = UNITS * it + UB[n] + u
                    t0 = max(0, (u - 4 * n) * P)
                    for h in range(2):
                        act.wait_ge(scores_up, 2 * unit + h + 1)
                        if clamp:
                            tile = s_ps[:, 2 * h:2 * h + 2, t0:t0 + P]
                            done = 4 * (4 * (4 * it + n) + u - 4 * n) + 2 * h
                            nc.scalar.activation(tile, tile, ACT.Relu, scale=-1.0).then_inc(clamped, 1)
                            act.wait_ge(clamped, done + 1)
                            nc.scalar.mul(tile, tile, -1.0).then_inc(clamped, 1)
                            act.wait_ge(clamped, done + 2)
                        at_least(act, pv_done, unit - PRING + 1)
                        nc.scalar.activation(pr[:, u % PRING, h, :, t0:], s_ps[:, 2 * h:2 * h + 2, t0:], ACT.Exp, scale=SCALE).then_inc(probs_ready, 1)

                def group(it, slot, rnd):
                    for n in range(NQ):
                        with act.If(slow > 0):
                            act.wait_ge(mt_parts, 12 * it + 3 * n + 3)
                            act.dma_start(rows_dram.rearrange("k (r t) -> r k t", t=P), nrow[:]).then_inc(m_out, 16)
                            act.wait_ge(m_out, 64 * it + 16 * n + 16)
                            act.dma_start(qs[ROWS:ROWS + NM, n], rows_dram.rearrange("k (j t) -> k j t", j=HG)).then_inc(m_rows, 16)
                        for u in range(4 * n):
                            exp(it, n, u, False)
                        with act.If(slow > 0):
                            for u in range(4 * n, 4 * n + 4):
                                exp(it, n, u, True)
                        with act.If(slow < 1):
                            for u in range(4 * n, 4 * n + 4):
                                exp(it, n, u, False)

                groups(act, group)

            @block.vector
            def _(dve):
                slow = dve.value_load(flag[0:1, 0:1], min_val=0, max_val=1)

                def maxima(it, n, slot):
                    bx = 4 * it + n
                    for i in range(TPB):
                        for j in range(HG):
                            dve.wait_ge(m_up, 16 * bx + 4 * i + j + 1)
                            width = (4 * n + i + 1) * P
                            ins = nc.vector.tensor_reduce(nmax[:, j * TPB + i:j * TPB + i + 1],
                                                          s_ps[:].rearrange("p a t -> p (a t)")[:, 0:width], AX.X, ALU.max, negate=True)
                            ins.then_inc(m_read, 1)
                    dve.wait_ge(mt_up, bx + 1)
                    at_least(dve, m_rows, 16 * bx)
                    turned = w_ps[0:HG * TPB, 0:P]
                    nc.vector.tensor_copy(nrow[:, 0], turned).then_inc(mt_parts, 1)
                    dve.wait_ge(mt_parts, 3 * bx + 1)
                    nc.vector.tensor_tensor(nsplit[:], turned, nrow[:, 0], ALU.subtract).then_inc(m_chain, 1)
                    dve.wait_ge(m_chain, bx + 1)
                    nc.vector.tensor_copy(nrow[:, 1], nsplit[:]).then_inc(mt_parts, 1)
                    dve.wait_ge(mt_parts, 3 * bx + 2)
                    nc.vector.tensor_tensor(nrow[:, 2], nsplit[:], nrow[:, 1], ALU.subtract).then_inc(mt_parts, 1)

                def o_evac(bx, par, unit_end):
                    dve.wait_ge(pv_done, unit_end)
                    nc.vector.tensor_copy(ot[:], o_ps[par][:]).then_inc(o_read, 1)

                def mask(unit, u, t0):
                    for h in range(2):
                        dve.wait_ge(probs_ready, 2 * unit + h + 1)
                        tile = pr[:, u % PRING, h, :, t0:t0 + P]
                        nc.vector.tensor_tensor(tile, tile, causal[:].unsqueeze(1).to_broadcast([P, 2, P]), ALU.min).then_inc(masked, 1)

                def task(name, bx, n, wn, xn_):
                    if name[0] == "A":
                        c = int(name[1])
                        dve.wait_ge(w_up, wn + 1)
                        nc.vector.tensor_tensor(am[:, n % 2, c], w_ps[:].rearrange("p (j t) -> p j t", j=HG),
                                                before[:].unsqueeze(1).to_broadcast([P, HG, P]), ALU.mult).then_inc(w_read, 1)
                    elif name == "T":
                        dve.wait_ge(w_up, wn + 1)
                        o4 = w_ps[:].rearrange("p (i j c) -> p i j c", i=TPB, j=HG)
                        at_least(dve, w_read, wn)
                        nc.vector.reciprocal(inv[:], o4[:, :, :, D]).then_inc(chain_s, 1)
                        dve.wait_ge(chain_s, 2 * bx + 1)
                        nc.vector.tensor_tensor(y[:], o4[:, :, :, 0:D], inv[:].unsqueeze(3).to_broadcast([P, TPB, HG, D]), ALU.mult).then_inc(w_read, 1)
                    elif name == "G":
                        dve.wait_ge(x_up, xn_ + 1)
                        at_least(dve, run_ready, 4 * bx)
                        nc.vector.tensor_tensor(gm[:], x_ps[0:CG].rearrange("p (i c) -> p i c", i=TPB),
                                                own[:].unsqueeze(1).to_broadcast([CG, TPB, P]), ALU.mult).then_inc(x_read, 1)
                        if n == 0:
                            nc.vector.memset(run[:, 0], 0.0).then_inc(chain_s, 1)
                        else:
                            nc.vector.tensor_copy(run[:, 0], run[:, TPB]).then_inc(chain_s, 1)
                        dve.wait_ge(x_read, xn_ + 1)
                        dve.wait_ge(chain_s, 2 * bx + 2)
                        for c in range(TPB):
                            if c:
                                dve.wait_ge(run_ready, 4 * bx + c)
                            nc.vector.tensor_tensor(run[:, c + 1], run[:, c], gm[:, c], ALU.add).then_inc(run_ready, 1)
                    elif name == "Y":
                        dve.wait_ge(x_up, xn_ + 1)
                        nc.vector.tensor_copy(y2t[:], x_ps[:]).then_inc(x_read, 1)
                    else:
                        dve.wait_ge(w_up, wn + 1)
                        grp = bx // 4
                        o4 = w_ps[:].rearrange("p (i j c) -> p i j c", i=TPB, j=HG)
                        out = z[:, ds(grp * (T // P) + 4 * n, TPB), :].rearrange("p i (j d) -> p i j d", d=D)
                        nc.vector.tensor_tensor(out, o4[:, :, :, 0:D], y[:], ALU.add).then_inc(w_read, 1)

                def group(it, slot, rnd):
                    for n in range(NQ):
                        bx = 4 * it + n
                        with dve.If(slow > 0):
                            maxima(it, n, slot)
                        for u in range(4 * n + 4):
                            if u == LAG - 1 and not (isinstance(bx, int) and bx == 0):
                                o_evac(bx - 1, (n - 1) % 2, UNITS * it + UB[n])
                            for step in tasks(it, UB[n] + u):
                                task(*step)
                            if u >= 4 * n:
                                mask(UNITS * it + UB[n] + u, u, (u - 4 * n) * P)

                groups(dve, group)
                o_evac(4 * NG - 1, 1, UNITS * NG)
                wn, xn_ = W_END, X_END
                for name in LAST:
                    task(name, 4 * NG - 1, NQ - 1, wn, xn_)
                    wn, xn_ = wn + (name in "TZ"), xn_ + (name in "GY")

            @block.tensor
            def _(pe):
                slow = pe.value_load(flag[0:1, 0:1], min_val=0, max_val=1)
                pe.wait_ge(pads_ready, 1)

                def maxima(it, n, slot):
                    bx = 4 * it + n
                    at_least(pe, probs_ready, 2 * (UNITS * it + UB[n]))
                    for i in range(TPB):
                        for j in range(HG):
                            at_least(pe, m_read, 16 * bx + 4 * i + j)
                            for blk in range(n + 1):
                                width = min(BLK, (4 * n + i + 1) * P - blk * BLK)
                                nc.tensor.matmul(s_ps[:, blk, 0:width], qs[0:ROWS, n, j, i * P:i * P + P],
                                                 ks[0:ROWS, slot, j, blk * BLK:blk * BLK + width], start=True, stop=(blk < n))
                            nc.tensor.matmul(s_ps[:, n, i * P:i * P + P], idb[:], later_t[:], start=False, stop=True).then_inc(m_up, 1)
                    pe.wait_ge(m_read, 16 * bx + 16)
                    at_least(pe, w_read, used(W_STEPS, it, sum(st[0] < UB[n] for st in SCHEDULE if st[1] not in ("G", "Y"))))
                    nc.tensor.transpose(w_ps[0:HG * TPB, 0:P], nmax[:], idf[:]).then_inc(mt_up, 1)
                    pe.wait_ge(m_rows, 16 * bx + 16)

                def scores(it, n, slot, u, h):
                    unit = UNITS * it + UB[n] + u
                    t0 = max(0, (u - 4 * n) * P)
                    at_least(pe, probs_ready, 2 * unit + h - 1)
                    for j in (2 * h, 2 * h + 1):
                        last = nc.tensor.matmul(s_ps[:, j, t0:], ks[:, slot, j, u * P:u * P + P], qs[:, n, j, t0:], start=True, stop=True)
                    last.then_inc(scores_up, 1)

                def values(it, n, slot, u):
                    unit = UNITS * it + UB[n] + u
                    t0 = max(0, (u - 4 * n) * P)
                    pe.wait_ge(probs_ready, 2 * unit + 2)
                    if u >= 4 * n:
                        pe.wait_ge(masked, 8 * (4 * it + n) + 2 * (u - 4 * n) + 2)
                    if u == 0:
                        at_least(pe, va_ready, it)
                        at_least(pe, o_read, 4 * it + n - 1)
                    for j in range(HG):
                        last = nc.tensor.matmul(o_ps[n % 2][PAD * j:PAD * (j + 1), t0:], va[:, slot, u, j], pr[:, u % PRING, j // 2, j % 2, t0:],
                                                start=(u == 0), stop=(u == 4 * n + 3), tile_position=(0, PAD * j), skip_group_check=True)
                    last.then_inc(pv_done, 1)

                def task(name, bx, n, wn, xn_):
                    if name[0] == "A":
                        c = int(name[1])
                        at_least(pe, w_read, wn)
                        if c == 0:
                            pe.wait_ge(as_in[n % 2], 96 * bx - 96 * (n % 2) + 192)
                        for j in range(HG):
                            last = nc.tensor.matmul(w_ps[:, j * P:j * P + P], kas[:, n % 2, j, c * P:c * P + P],
                                                    qas[:, n % 2, j, c * P:c * P + P], start=True, stop=True)
                        last.then_inc(w_up, 1)
                    elif name in "TZ":
                        src = ot if name == "T" else y2t
                        if name == "T":
                            pe.wait_ge(o_read, bx + 1)
                        else:
                            pe.wait_ge(x_read, xn_)
                        at_least(pe, w_read, wn)
                        for i in range(TPB):
                            last = nc.tensor.transpose(w_ps[:, i * P:i * P + P], src[:, i * P:i * P + P], idf[:])
                        last.then_inc(w_up, 1)
                    elif name == "G":
                        pe.wait_ge(e_ready, bx + 1)
                        pe.wait_ge(lin_in[n % 2], 24 * bx - 24 * (n % 2) + 48)
                        at_least(pe, x_read, xn_)
                        for c in range(TPB):
                            last = nc.tensor.matmul(x_ps[0:CG, c * P:c * P + P], kan[:, n % 2, c], e[:, c].rearrange("p j d -> p (j d)"), start=True, stop=True)
                        last.then_inc(x_up, 1)
                    else:
                        pe.wait_ge(run_ready, 4 * bx + 4)
                        pe.wait_ge(x_read, xn_)
                        pe.wait_ge(w_read, wn)
                        for c in range(TPB):
                            nc.tensor.matmul(x_ps[:, c * P:c * P + P], run[:, c], qap[:, n % 2, c * P:c * P + P], start=(c == 0), stop=False, skip_group_check=True)
                        for c in range(TPB):
                            for j in range(HG):
                                last = nc.tensor.matmul(x_ps[PAD * j:PAD * (j + 1), c * P:c * P + P], e[:, c, j], am[:, n % 2, c, j],
                                                        start=False, stop=(c == TPB - 1), tile_position=(0, PAD * j), skip_group_check=True)
                        last.then_inc(x_up, 1)

                def group(it, slot, rnd):
                    first = isinstance(it, int) and it == 0
                    if not first:
                        pe.wait_ge(ks_in[slot], 96 * rnd + 96 * slot)
                    for n in range(NQ):
                        bx = 4 * it + n
                        if first and n >= EARLY:
                            pe.wait_ge(ks_first[n], 96)
                        at_least(pe, qs_in[n], 96 * it + (96 if n >= EARLY else 0))
                        with pe.If(slow > 0):
                            maxima(it, n, slot)
                        for u in range(4 * n + 4):
                            scores(it, n, slot, u, 0)
                            if u >= LAG:
                                values(it, n, slot, u - LAG)
                            elif n:
                                values(it, n - 1, slot, 4 * n + u - LAG)
                            elif not (isinstance(it, int) and it == 0):
                                values(it - 1, NQ - 1, 1 - slot, 4 * NQ + u - LAG)
                            scores(it, n, slot, u, 1)
                            for step in tasks(it, UB[n] + u):
                                task(*step)

                groups(pe, group)
                for u in range(4 * NQ - LAG, 4 * NQ):
                    values(NG - 1, NQ - 1, 1, u)
                wn, xn_ = W_END, X_END
                for name in LAST:
                    task(name, 4 * NG - 1, NQ - 1, wn, xn_)
                    wn, xn_ = wn + (name in "TZ"), xn_ + (name in "GY")


BETWEEN = [1, 2, 4, 10, 10, 2]
BEFORE_LOW = 2
TURN_Z, PROJECT = 3, 5


def finish(nc, t, sh):
    idf, z, x, out = sh.idf, sh.z, t["x"], t["out"]
    with ExitStack() as ctx:
        sb = lambda name, shape, dt: ctx.enter_context(nc.sbuf_tensor(name, shape, dt))
        ps = lambda name, shape: ctx.enter_context(nc.psum_tensor(name, shape, F32))
        sem = lambda name: ctx.enter_context(nc.semaphore(name))
        wp = sb("w_proj_sb", [P, KT, C], F32)
        wi = sb("w_int", [P, 3, KT * HID], I32)
        wg = sb("w_gate_sb", [P, KT, HID], F16)
        wu = sb("w_up_sb", [P, KT, HID], F16)
        wd = sb("w_down_sb", [P, NH, C], F16)
        x4 = sb("x_again", [P, TPB, C], F32)
        x1 = sb("x1", [P, NTOK // P, C], F32)
        zs = sb("z_block", [P, TPB, C], F32)
        zt = sb("z_t", [P, KT, BLK], F32)
        a = sb("attended", [P, TPB, C], F32)
        xs = sb("x1n_block", [P, TPB, C], F32)
        xh = sb("x1n_t_hi", [P, KT, BLK], F16)
        xl = sb("x1n_t_lo", [P, KT, BLK], F16)
        sg = sb("silu_gate", [P, 2, BLK], F32)
        h = sb("half_hidden", [P, NH, BLK], F32)
        hh = sb("half_hidden_hi", [P, NH, BLK], F16)
        hl = sb("half_hidden_lo", [P, NH, BLK], F16)
        f = sb("fed", [P, TPB, C], F32)
        yo = sb("out_block", [P, TPB, C], F32)
        st = [sb(f"st_c{i}", [P, TPB, 6], F32) for i in range(3)]
        mv = [sb(f"mv_c{i}", [P, TPB, 2], F32) for i in range(3)]
        nt = [[sb(f"nt_c{i}{k}", [P, TPB], F32) for k in range(3)] for i in range(3)]
        t_ps = ps("t_ps", [P, KT, BLK])
        a_ps = ps("a_ps", [P, TPB, C])
        g_ps = ps("g_ps", [P, 2, BLK])
        u_ps = ps("up_ps", [P, 2, BLK])

        idle = sem("idle_c")
        fp_in, int_in, w_ready = sem("fp_in"), [sem(f"int_in{i}") for i in range(3)], sem("w_ready")
        x_in, z_ready, z_up, zt_ready, a_up, a_ready = sem("x_again_in"), sem("zs_ready"), sem("z_up"), sem("zt_ready"), sem("a_up"), sem("a_ready")
        a_normed, x1_ready, xs_ready, xt_up, hi_ready, lo_ready = sem("a_normed"), sem("x1_ready"), sem("xs_ready"), sem("x1t_up"), sem("x1_hi"), sem("x1_lo")
        hh_ready, hl_ready = sem("hh_ready"), sem("hl_ready")
        gu_up, silu_ready, h_ready, f_up, f_ready, f_normed = sem("gu_up"), sem("silu_ready"), sem("h_ready"), sem("f_up"), sem("f_ready"), sem("f_normed")
        out_ready, stored = sem("out_ready"), sem("out_stored")
        chains = [sem(f"chain_c{i}") for i in range(3)]

        def at_least(engine, s, value):
            if not isinstance(value, int) or value > 0:
                engine.wait_ge(s, value)

        def blocks(engine, body):
            body(0, 2)
            with engine.Fori(1, NBLK - 2) as n:
                body(n, 2)
            body(NBLK - 2, 1)
            body(NBLK - 1, 0)

        def z_of(n, g):
            return z[:, ds((n // NQ * NG_B + g) * (T // P) + n % NQ * TPB, TPB), :]

        def rows(dram, n):
            return dram[ds(n * BLK, BLK), :].rearrange("(i p) c -> p i c", p=P)

        with nc.Block() as block:

            @block.sync
            def _(sp):
                def load_x(n):
                    hold(sp, x1_ready, n, idle)
                    sp.dma_start(x4[:], rows(x, n)).then_inc(x_in, 16)

                def store(n):
                    hold(sp, out_ready, n + 1, idle)
                    sp.dma_start(rows(out, n), yo[:]).then_inc(stored, 16)

                def body(n, ahead):
                    if ahead == 2:
                        load_x(n + 2)
                    if not (isinstance(n, int) and n == 0):
                        store(n - 1)

                sp.dma_start(wp[:], t["w_proj"].rearrange("(k p) m -> p k m", p=P)).then_inc(fp_in, 16)
                load_x(0)
                for i, (w, k) in enumerate(((t["w_gate"], KT), (t["w_up"], KT), (t["w_down"], NH))):
                    sp.dma_start(wi[:, i].rearrange("p (k m) -> p k m", k=k), w.rearrange("(k p) m -> p k m", p=P)).then_inc(int_in[i], 16)
                load_x(1)
                blocks(sp, body)
                store(NBLK - 1)
                sp.wait_ge(stored, 16 * NBLK)

            @block.gpsimd
            def _(pool):
                def stage_z(n):
                    hold(pool, z_up, n, idle)
                    for g in range(NG_B):
                        nc.gpsimd.tensor_copy(zs[:, :, g * CG:(g + 1) * CG], z_of(n, g)).then_inc(z_ready, 1)

                def total(n):
                    pool.wait_ge(f_normed, 4 * n + 4)
                    at_least(pool, stored, 16 * n)
                    nc.gpsimd.tensor_tensor(yo[:], f[:], x1[:, ds(n * TPB, TPB), :], ALU.add).then_inc(out_ready, 1)

                def body(n, ahead):
                    if ahead == 2:
                        stage_z(n + 2)
                    for m in range(NH):
                        pool.wait_ge(hh_ready, NH * n + m + 1)
                        at_least(pool, f_up, n)
                        nc.gpsimd.tensor_tensor(hl[:, m], h[:, m], hh[:, m], ALU.subtract).then_inc(hl_ready, 1)
                    if not (isinstance(n, int) and n == 0):
                        total(n - 1)

                stage_z(1)
                blocks(pool, body)

            @block.scalar
            def _(act):
                def weights(dst, i):
                    act.wait_ge(int_in[i], 16)
                    nc.scalar.copy(dst[:].rearrange("p k m -> p (k m)"), wi[:, i]).then_inc(w_ready, 1)

                def z_turned(n):
                    act.wait_ge(z_up, n + 1)
                    at_least(act, a_up, n)
                    nc.scalar.copy(zt[:], t_ps[:]).then_inc(zt_ready, 1)

                def attended(n):
                    act.wait_ge(a_up, n + 1)
                    at_least(act, x1_ready, n)
                    nc.scalar.copy(a[:], a_ps[:]).then_inc(a_ready, 1)

                def x_turned(n):
                    act.wait_ge(xt_up, n + 1)
                    at_least(act, gu_up, NH * n)
                    nc.scalar.copy(xh[:], t_ps[:]).then_inc(hi_ready, 1)

                def hidden_hi(n, m):
                    act.wait_ge(h_ready, NH * n + m + 1)
                    at_least(act, f_up, n)
                    nc.scalar.copy(hh[:, m], h[:, m]).then_inc(hh_ready, 1)

                def body(n, ahead):
                    for m in range(NH):
                        act.wait_ge(gu_up, NH * n + m + 1)
                        at_least(act, h_ready, NH * n + m - 1)
                        nc.scalar.activation(sg[:, m % 2], g_ps[:, m % 2], ACT.Silu, scale=WSCALE).then_inc(silu_ready, 1)
                        if m:
                            hidden_hi(n, m - 1)
                        if ahead == 2 and m == TURN_Z:
                            z_turned(n + 2)
                        if ahead == 2 and m == PROJECT:
                            attended(n + 2)
                    hidden_hi(n, NH - 1)
                    if ahead:
                        x_turned(n + 1)
                    act.wait_ge(f_up, n + 1)
                    at_least(act, out_ready, n)
                    nc.scalar.mul(f[:], a_ps[:], 2 * WSCALE).then_inc(f_ready, 1)

                z_turned(0)
                attended(0)
                z_turned(1)
                weights(wg, 0)
                weights(wu, 1)
                attended(1)
                x_turned(0)
                weights(wd, 2)
                blocks(act, body)

            @block.vector
            def _(dve):
                def normed(dst, src, which, i):
                    return nc.vector.tensor_scalar(dst, src, mv[which][:, i, 0:1], mv[which][:, i, 1:2], ALU.subtract, ALU.mult)

                def tile_of_x1(n, i):
                    return x1[:, ds(n * TPB + i, 1), :].rearrange("p a c -> p (a c)")

                def residual(n):
                    dve.wait_ge(a_ready, n + 1)
                    yield from ln_moments(nc, dve, chains[0], LN_STEPS * n, [a[:, i, :] for i in range(TPB)], st[0], mv[0], idle)
                    yield
                    yield from ln_rsqrt(nc, dve, chains[0], LN_STEPS * n, mv[0], nt[0])
                    dve.wait_ge(chains[0], LN_STEPS * n + LN_STEPS)
                    for i in range(TPB):
                        normed(a[:, i, :], a[:, i, :], 0, i).then_inc(a_normed, 1)
                    dve.wait_ge(a_normed, 4 * n + 4)
                    dve.wait_ge(x_in, 16 * n + 16)
                    nc.vector.tensor_tensor(x1[:, ds(n * TPB, TPB), :], x4[:], a[:], ALU.add).then_inc(x1_ready, 1)

                def second_norm(n):
                    hold(dve, x1_ready, n + 1, idle)
                    yield from ln_moments(nc, dve, chains[1], LN_STEPS * n, [tile_of_x1(n, i) for i in range(TPB)], st[1], mv[1], idle)
                    yield
                    yield from ln_rsqrt(nc, dve, chains[1], LN_STEPS * n, mv[1], nt[1])
                    dve.wait_ge(chains[1], LN_STEPS * n + LN_STEPS)
                    at_least(dve, xt_up, n)
                    for i in range(TPB):
                        if i == TPB // 2:
                            yield
                        normed(xs[:, i, :], tile_of_x1(n, i), 1, i).then_inc(xs_ready, 1)

                def low_part(n):
                    dve.wait_ge(hi_ready, n + 1)
                    at_least(dve, gu_up, NH * n)
                    nc.vector.tensor_tensor(xl[:], t_ps[:], xh[:], ALU.subtract).then_inc(lo_ready, 1)

                def last_norm(n):
                    dve.wait_ge(f_ready, n + 1)
                    yield from ln_moments(nc, dve, chains[2], LN_STEPS * n, [f[:, i, :] for i in range(TPB)], st[2], mv[2], idle)
                    yield
                    yield from ln_rsqrt(nc, dve, chains[2], LN_STEPS * n, mv[2], nt[2])
                    dve.wait_ge(chains[2], LN_STEPS * n + LN_STEPS)
                    for i in range(TPB):
                        if i == TPB // 2:
                            yield
                        normed(f[:, i, :], f[:, i, :], 2, i).then_inc(f_normed, 1)

                def body(n, ahead):
                    first = isinstance(n, int) and n == 0
                    between = by_turns(*([second_norm(n + 1)] if ahead else []) + ([] if first else [last_norm(n - 1)]))
                    for m in range(NH):
                        dve.wait_ge(silu_ready, NH * n + m + 1)
                        at_least(dve, hl_ready, NH * (n - 1) + m + 1)
                        nc.vector.scalar_tensor_tensor(h[:, m], u_ps[:, m % 2], WSCALE / 2, sg[:, m % 2], ALU.mult, ALU.mult).then_inc(h_ready, 1)
                        for _ in range(BETWEEN[m]):
                            next(between, None)
                    run_all(between)
                    other = residual(n + 2) if ahead == 2 else iter(())
                    for _ in range(BEFORE_LOW):
                        next(other, None)
                    if ahead:
                        low_part(n + 1)
                    run_all(other)

                for g in range(NG_B):
                    nc.vector.tensor_copy(zs[:, :, g * CG:(g + 1) * CG], z_of(0, g)).then_inc(z_ready, 1)
                run_all(residual(0))
                run_all(second_norm(0))
                low_part(0)
                run_all(residual(1))
                blocks(dve, body)
                run_all(last_norm(NBLK - 1))
                dve.wait_ge(f_normed, 4 * NBLK)
                dve.wait_ge(stored, 16 * (NBLK - 1))
                nc.vector.tensor_tensor(yo[:], f[:], x1[:, (NBLK - 1) * TPB:, :], ALU.add).then_inc(out_ready, 1)

            @block.tensor
            def _(pe):
                def turn_z(n):
                    pe.wait_ge(z_ready, 4 * n + 4)
                    if isinstance(n, int) and n < 2:
                        at_least(pe, zt_ready, n)
                    else:
                        pe.wait_ge(lo_ready, n - 1)
                    for i in range(TPB):
                        for k in range(KT):
                            last = nc.tensor.transpose(t_ps[:, k, i * P:i * P + P], zs[:, i, k * P:k * P + P], idf[:])
                    last.then_inc(z_up, 1)

                def project_z(n):
                    pe.wait_ge(zt_ready, n + 1)
                    at_least(pe, a_ready, n)
                    if not (isinstance(n, int) and n < 3):
                        pe.wait_ge(f_ready, n - 2)
                    for i in range(TPB):
                        for k in range(KT):
                            last = nc.tensor.matmul(a_ps[:, i], zt[:, k, i * P:i * P + P], wp[:, k], start=(k == 0), stop=(k == KT - 1))
                    last.then_inc(a_up, 1)

                def turn_x(n):
                    pe.wait_ge(xs_ready, 4 * n + 4)
                    for i in range(TPB):
                        for k in range(KT):
                            last = nc.tensor.transpose(t_ps[:, k, i * P:i * P + P], xs[:, i, k * P:k * P + P], idf[:])
                    last.then_inc(xt_up, 1)

                def body(n, ahead):
                    pe.wait_ge(lo_ready, n + 1)
                    for m in range(NH):
                        at_least(pe, h_ready, NH * n + m - 1)
                        for w, bank in ((wg, g_ps), (wu, u_ps)):
                            for k in range(KT):
                                for part in (xh, xl):
                                    last = nc.tensor.matmul(bank[:, m % 2], w[:, k, m * P:m * P + P], part[:, k],
                                                            start=(k == 0 and part is xh), stop=(k == KT - 1 and part is xl))
                        last.then_inc(gu_up, 1)
                        if ahead == 2 and m == TURN_Z:
                            turn_z(n + 2)
                        if ahead == 2 and m == PROJECT:
                            project_z(n + 2)
                    if ahead:
                        turn_x(n + 1)
                    pe.wait_ge(hl_ready, NH * n + NH)
                    pe.wait_ge(a_ready, n + 1 + ahead)
                    for i in range(TPB):
                        for k in range(NH):
                            for part in (hh, hl):
                                last = nc.tensor.matmul(a_ps[:, i], part[:, k, i * P:i * P + P], wd[:, k],
                                                        start=(k == 0 and part is hh), stop=(k == NH - 1 and part is hl))
                    last.then_inc(f_up, 1)

                pe.wait_ge(fp_in, 16)
                for n in range(2):
                    turn_z(n)
                    project_z(n)
                turn_x(0)
                pe.wait_ge(w_ready, 3)
                blocks(pe, body)


class Shared:
    pass


def layer(nc, t):
    parts = nc.dram_tensor("parts_dram", (4, 3, B * C, T), BF16, kind="Internal").ap()
    qa32 = nc.dram_tensor("qa32_dram", (B * C, T), F32, kind="Internal").ap()
    ka_nat = nc.dram_tensor("ka_nat_dram", (NTOK, C), F32, kind="Internal").ap()
    xn_dram = nc.dram_tensor("xn_dram", (NTOK + 1, C), F32, kind="Internal").ap()
    rows_dram = nc.dram_tensor("minus_max_dram", (NM, HG * BLK), BF16, kind="Internal").ap()
    with ExitStack() as outer, ExitStack() as ctx:
        sb = lambda name, shape, dt: ctx.enter_context(nc.sbuf_tensor(name, shape, dt))
        sh = Shared()
        keep = lambda name, shape, dt: outer.enter_context(nc.sbuf_tensor(name, shape, dt))
        sh.flag = keep("flag", [1, 1], I32)
        sh.z = keep("z", [P, NG * T // P, CG], F32)
        sh.idf = keep("ident_f", [P, P], F32)
        sh.idb = sb("ident_b", [P, P], BF16)
        sh.causal = sb("causal", [P, P], F32)
        sh.later_t = sb("later_keys_t", [P, P], BF16)
        sh.before = sb("before", [P, P], F32)
        sh.own = sb("own_head", [CG, P], F32)
        sh.ks = sb("k_stack", [ROWS + NM, 2, HG, T], BF16)
        sh.qs = sb("q_stack", [ROWS + NM, NQ, HG, BLK], BF16)
        sh.vraw = sb("v_raw", [P, T // P, CG], F32)
        sh.va = sb("v_and_one", [P, 2, T // P, HG, PAD], F32)
        project(nc, t, sh, parts, qa32, ka_nat, xn_dram)
        attend(nc, sh, parts, qa32, ka_nat, xn_dram, rows_dram)
        ctx.close()
        finish(nc, t, sh)


def kernel(**inputs):
    import ml_dtypes
    import numpy as np
    import concourse.bacc as bacc
    from concourse.bass_utils import run_bass_kernel_spmd

    bf16 = ml_dtypes.bfloat16
    i = np.arange(P)
    own = np.zeros((CG, P), np.float32)
    for j in range(HG):
        own[j * D:(j + 1) * D, j * PAD:j * PAD + D] = 1
    arrays = {
        "x": np.ascontiguousarray(inputs["L0_attn_x"]).reshape(NTOK, C),
        "w_attn": np.ascontiguousarray(inputs["L0_attn_W_attn"]),
        "w_k2": np.ascontiguousarray(inputs["L0_attn_W_k2"]),
        "w_proj": np.ascontiguousarray(inputs["L0_attn_W_proj"]),
        "w_gate": np.ascontiguousarray(np.asarray(inputs["L0_ffn_w_gate"]).T),
        "w_up": np.ascontiguousarray(np.asarray(inputs["L0_ffn_w_up"]).T),
        "w_down": np.ascontiguousarray(np.asarray(inputs["L0_ffn_w_down"]).T),
        "ident": np.eye(P, dtype=np.float32),
        "ident_bf": np.eye(P).astype(bf16),
        "heads": np.repeat(np.eye(P // D, dtype=np.float32), D, axis=0),
        "causal": np.where(i[:, None] > i[None, :], 0.0, np.finfo(np.float32).max).astype(np.float32),
        "later_t": np.where(i[:, None] < i[None, :], NEG, 0.0).astype(bf16),
        "before": (i[:, None] < i[None, :]).astype(np.float32),
        "own": own,
    }
    nc = bacc.Bacc("TRN2", target_bir_lowering=False, num_devices=1)
    t = {name: nc.dram_tensor(f"in_{name}", a.shape, mybir.dt.from_np(a.dtype), kind="ExternalInput").ap()
         for name, a in arrays.items()}
    t["out"] = nc.dram_tensor("out", (NTOK, C), F32, kind="ExternalOutput").ap()
    layer(nc, t)
    r = run_bass_kernel_spmd(nc, [{f"in_{name}": a for name, a in arrays.items()}], core_ids=[0])
    return r.results[0]["out"].reshape(B, T, C)
```
